# Optimizing a Trainium2 kernel written in Bass

```python
import numpy as np
import jax
import jax.numpy as jnp

def _softmax(x, axis=-1):
    return jax.nn.softmax(x, axis=axis)

def _gelu(x):
    return jax.nn.gelu(x, approximate=True)

def _silu(x):
    return jax.nn.silu(x)

def _sigmoid(x):
    return jax.nn.sigmoid(x)

def _layernorm(x, axis=-1, eps=1e-05):
    m = jnp.mean(x, axis=axis, keepdims=True)
    v = jnp.var(x, axis=axis, keepdims=True)
    return (x - m) / jnp.sqrt(v + eps)

def _scatter_add(tgt, idx, src, axis=0):
    return tgt.at[idx].add(src)

def _segment_sum(src, seg, n):
    return jax.ops.segment_sum(src, seg, n)
kernel_name = 'mk_xattn_seq_d2_seqx_r8_e36e69'

def setup_inputs(seed: int=0):
    np.random.seed(seed)
    _w = jnp.asarray

    def _rec_inputs():
        import jax
        import jax.numpy as jnp
        _rk = jax.random.key(seed)
        x = -0.0002928 + 1 * jax.random.normal(jax.random.fold_in(_rk, 1), (64, 128, 128), jnp.float32)
        _lenS = 128 - jax.random.randint(jax.random.fold_in(_rk, 7), (64,), 0, max(1, 128 // 4) + 1, jnp.int32)
        _lenS2 = 77 - jax.random.randint(jax.random.fold_in(_rk, 8), (64,), 0, max(1, 77 // 4) + 1, jnp.int32)
        _ctx_1024P = jax.random.normal(jax.random.fold_in(_rk, 11), (64, 16, 128), jnp.float32)
        _ctx_1024c = jax.random.dirichlet(jax.random.fold_in(_rk, 511), 0.3 * jnp.ones((16,), jnp.float32), (64, 77))
        _ctx_1024t = jnp.einsum('bsk,bkd->bsd', _ctx_1024c, _ctx_1024P)
        _ctx_1024t = _ctx_1024t * jax.lax.rsqrt(jnp.mean(jnp.square(_ctx_1024t)) + 1e-12) * 0.953939
        ctx_1024 = -1.39393e-06 + 0.999914 * (_ctx_1024t + 0.3 * jax.random.normal(jax.random.fold_in(_rk, 611), (64, 77, 128), jnp.float32))
        _validS = jnp.arange(128)[None, :] < _lenS[:, None]
        _validS2 = jnp.arange(77)[None, :] < _lenS2[:, None]
        _causal = jnp.tril(jnp.ones((128, 128), dtype=bool))
        mask_Bx1xSxS2_fk0 = jnp.where(jnp.broadcast_to(_validS2[:, None, None, :], (64, 1, 128, 77)), 0.0, 1.0).astype(jnp.float32)
        return (x, ctx_1024, mask_Bx1xSxS2_fk0)
    x, ctx_1024, mask_Bx1xSxS2_fk0 = _rec_inputs()

    def _L0_xattn_setup():
        import jax, jax.numpy as jnp
        import numpy as np
        ALPHA = 0.5
        SCORES_CLAMP = 50.0
        LN_EPS = 1e-05
        N_HEADS = 16
        key = jax.random.key(seed)
        ks = jax.random.split(key, 16)
        B, Q, K, D = (2, 256, 256, 128)
        s = 1.0 / np.sqrt(D)
        return {'query': jax.random.normal(ks[0], (B, Q, D), jnp.float32), 'key_in': jax.random.normal(ks[1], (B, K, D), jnp.float32), 'mask': jax.random.randint(ks[2], (B, 1, Q, K), 0, 2).astype(jnp.float32), 'Wq': jax.random.normal(ks[3], (D, D), jnp.float32) * s, 'bq': jnp.zeros((D,), jnp.float32), 'Wk': jax.random.normal(ks[4], (D, D), jnp.float32) * s, 'bk': jnp.zeros((D,), jnp.float32), 'Wv': jax.random.normal(ks[5], (D, D), jnp.float32) * s, 'bv': jnp.zeros((D,), jnp.float32), 'Wo': jax.random.normal(ks[6], (D, D), jnp.float32) * s, 'bo': jnp.zeros((D,), jnp.float32), 'gamma': jnp.ones((D,), jnp.float32), 'beta': jnp.zeros((D,), jnp.float32)}
    _L0_xattn_all = _L0_xattn_setup()
    _L0_xattn_in = {k: v for k, v in _L0_xattn_all.items() if k in ('Wq', 'bq', 'Wk', 'bk', 'Wv', 'bv', 'Wo', 'bo', 'gamma', 'beta')}
    del _L0_xattn_all

    def _L1_xattn_setup():
        import jax, jax.numpy as jnp
        import numpy as np
        B, N, DIM = (2, 256, 128)
        HEADS, DH = (16, 64)
        SEG = 64
        NPM = 16
        NM = 16
        DFF = int(DIM * 4 * 2 / 3)
        EPS = 1.1920929e-07

        def rms_norm(x, w):
            return x * jax.lax.rsqrt(jnp.mean(x * x, axis=-1, keepdims=True) + EPS) * w
        key = jax.random.key(seed)
        ks = jax.random.split(key, 10)
        p = lambda i, shape: jax.random.normal(ks[i], shape, jnp.float32) * 0.02
        return {'x': jax.random.normal(ks[0], (B, N, DIM), jnp.float32), 'mem_out': jax.random.normal(ks[1], (B, N, DIM), jnp.float32), 'attn_norm_w': jnp.ones((DIM,), jnp.float32), 'to_qkv_w': p(2, (DIM, 3 * HEADS * DH)), 'to_out_w': p(3, (HEADS * DH, DIM)), 'persist_mem': jax.random.normal(ks[4], (HEADS, NPM, DH), jnp.float32), 'mem_pool_norm_w': jnp.ones((DIM,), jnp.float32), 'to_mem_tokens_w': p(5, (DIM, DIM)), 'ff_norm_w': jnp.ones((DIM,), jnp.float32), 'ff_w1': p(6, (DIM, 2 * DFF)), 'ff_b1': jnp.zeros((2 * DFF,), jnp.float32), 'ff_w2': p(7, (DFF, DIM)), 'ff_b2': jnp.zeros((DIM,), jnp.float32)}
    _L1_xattn_all = _L1_xattn_setup()
    _L1_xattn_in = {k: v for k, v in _L1_xattn_all.items() if k in ('attn_norm_w', 'to_qkv_w', 'to_out_w', 'persist_mem', 'mem_pool_norm_w', 'to_mem_tokens_w', 'ff_norm_w', 'ff_w1', 'ff_b1', 'ff_w2', 'ff_b2')}
    del _L1_xattn_all
    return {'x': x, 'ctx_1024': ctx_1024, 'mask_Bx1xSxS2_fk0': mask_Bx1xSxS2_fk0, 'L0_xattn_Wq': _L0_xattn_in['Wq'], 'L0_xattn_bq': _L0_xattn_in['bq'], 'L0_xattn_Wk': _L0_xattn_in['Wk'], 'L0_xattn_bk': _L0_xattn_in['bk'], 'L0_xattn_Wv': _L0_xattn_in['Wv'], 'L0_xattn_bv': _L0_xattn_in['bv'], 'L0_xattn_Wo': _L0_xattn_in['Wo'], 'L0_xattn_bo': _L0_xattn_in['bo'], 'L0_xattn_gamma': _L0_xattn_in['gamma'], 'L0_xattn_beta': _L0_xattn_in['beta'], 'L1_xattn_attn_norm_w': _L1_xattn_in['attn_norm_w'], 'L1_xattn_to_qkv_w': _L1_xattn_in['to_qkv_w'], 'L1_xattn_to_out_w': _L1_xattn_in['to_out_w'], 'L1_xattn_persist_mem': _L1_xattn_in['persist_mem'], 'L1_xattn_mem_pool_norm_w': _L1_xattn_in['mem_pool_norm_w'], 'L1_xattn_to_mem_tokens_w': _L1_xattn_in['to_mem_tokens_w'], 'L1_xattn_ff_norm_w': _L1_xattn_in['ff_norm_w'], 'L1_xattn_ff_w1': _L1_xattn_in['ff_w1'], 'L1_xattn_ff_b1': _L1_xattn_in['ff_b1'], 'L1_xattn_ff_w2': _L1_xattn_in['ff_w2'], 'L1_xattn_ff_b2': _L1_xattn_in['ff_b2']}

def reference(x, ctx_1024, mask_Bx1xSxS2_fk0, L0_xattn_Wq, L0_xattn_bq, L0_xattn_Wk, L0_xattn_bk, L0_xattn_Wv, L0_xattn_bv, L0_xattn_Wo, L0_xattn_bo, L0_xattn_gamma, L0_xattn_beta, L1_xattn_attn_norm_w, L1_xattn_to_qkv_w, L1_xattn_to_out_w, L1_xattn_persist_mem, L1_xattn_mem_pool_norm_w, L1_xattn_to_mem_tokens_w, L1_xattn_ff_norm_w, L1_xattn_ff_w1, L1_xattn_ff_b1, L1_xattn_ff_w2, L1_xattn_ff_b2):
    import jax
    import jax.numpy as jnp

    def _L0_xattn_ref(query, key_in, mask, Wq, bq, Wk, bk, Wv, bv, Wo, bo, gamma, beta):
        import jax, jax.numpy as jnp
        import numpy as np
        ALPHA = 0.5
        SCORES_CLAMP = 50.0
        LN_EPS = 1e-05
        N_HEADS = 16
        B, Qlen, D = query.shape
        Klen = key_in.shape[1]
        H = N_HEADS
        hd = D // H
        q = (query @ Wq + bq).reshape(B, Qlen, H, hd).transpose(0, 2, 1, 3)
        k = (key_in @ Wk + bk).reshape(B, Klen, H, hd).transpose(0, 2, 1, 3)
        v = (key_in @ Wv + bv).reshape(B, Klen, H, hd).transpose(0, 2, 1, 3)
        scores = jnp.einsum('bhqd,bhkd->bhqk', q, k) / jnp.sqrt(jnp.float32(hd))
        scores = ALPHA * (scores * mask) + (1.0 - ALPHA) * scores
        scores = jnp.clip(scores, -SCORES_CLAMP, SCORES_CLAMP)
        attn = jax.nn.softmax(scores, axis=-1)
        context = jnp.einsum('bhqk,bhkd->bhqd', attn, v)
        context = context.transpose(0, 2, 1, 3).reshape(B, Qlen, D)
        out = context @ Wo + bo
        resid = query + out
        mu = jnp.mean(resid, axis=-1, keepdims=True)
        var = jnp.mean(jnp.square(resid - mu), axis=-1, keepdims=True)
        return (resid - mu) * jax.lax.rsqrt(var + LN_EPS) * gamma + beta

    def _L1_xattn_ref(x, mem_out, attn_norm_w, to_qkv_w, to_out_w, persist_mem, mem_pool_norm_w, to_mem_tokens_w, ff_norm_w, ff_w1, ff_b1, ff_w2, ff_b2):
        import jax, jax.numpy as jnp
        import numpy as np
        B, N, DIM = (2, 256, 128)
        HEADS, DH = (16, 64)
        SEG = 64
        NPM = 16
        NM = 16
        DFF = int(DIM * 4 * 2 / 3)
        EPS = 1.1920929e-07

        def rms_norm(x, w):
            return x * jax.lax.rsqrt(jnp.mean(x * x, axis=-1, keepdims=True) + EPS) * w
        b, n, _ = x.shape
        split_heads = lambda t: t.reshape(b, -1, HEADS, DH).transpose(0, 2, 1, 3)
        pooled = rms_norm(mem_out.mean(axis=1), mem_pool_norm_w)
        mem_tok = jnp.broadcast_to((pooled @ to_mem_tokens_w)[:, None, :], (b, NM, DIM))
        _, k_c, v_c = jnp.split(mem_tok @ to_qkv_w, 3, axis=-1)
        k_extra, v_extra = (split_heads(k_c), split_heads(v_c))
        xn = rms_norm(x, attn_norm_w)
        q, k, v = jnp.split(xn @ to_qkv_w, 3, axis=-1)
        q, k, v = (split_heads(q), split_heads(k), split_heads(v))
        pos = jnp.arange(n)
        inv = 1.0 / 10000.0 ** (jnp.arange(0, DH, 2, dtype=jnp.float32) / DH)
        ang = jnp.repeat(pos[:, None].astype(jnp.float32) * inv[None, :], 2, axis=-1)
        cos, sin = (jnp.cos(ang), jnp.sin(ang))

        def rope(t):
            z = t.reshape(t.shape[:-1] + (-1, 2))
            rh = jnp.stack([-z[..., 1], z[..., 0]], axis=-1).reshape(t.shape)
            return t * cos + rh * sin
        q, k = (rope(q), rope(k))
        pm = jnp.broadcast_to(persist_mem[None], (b, HEADS, NPM, DH))
        kf = jnp.concatenate([k_extra, pm, k], axis=2)
        vf = jnp.concatenate([v_extra, pm, v], axis=2)
        P = NPM + NM
        ki = jnp.arange(kf.shape[2])[None, :]
        qi = pos[:, None]
        causal = qi >= ki - P
        seg = qi // SEG == (ki - P) // SEG
        mask = causal & seg | (ki < P)
        scores = jnp.einsum('bhid,bhjd->bhij', q, kf) * DH ** (-0.5)
        scores = jnp.where(mask[None, None], scores, -1e+30)
        probs = jax.nn.softmax(scores, axis=-1)
        o = jnp.einsum('bhij,bhjd->bhid', probs, vf)
        attn_out = o.transpose(0, 2, 1, 3).reshape(b, n, HEADS * DH) @ to_out_w
        x = x + attn_out
        h = rms_norm(x, ff_norm_w) @ ff_w1 + ff_b1
        a, g = jnp.split(h, 2, axis=-1)
        x = x + jax.nn.silu(g) * a @ ff_w2 + ff_b2
        return x
    x = _L0_xattn_ref(x, ctx_1024, mask_Bx1xSxS2_fk0, L0_xattn_Wq, L0_xattn_bq, L0_xattn_Wk, L0_xattn_bk, L0_xattn_Wv, L0_xattn_bv, L0_xattn_Wo, L0_xattn_bo, L0_xattn_gamma, L0_xattn_beta)
    x = _L1_xattn_ref(x, ctx_1024, L1_xattn_attn_norm_w, L1_xattn_to_qkv_w, L1_xattn_to_out_w, L1_xattn_persist_mem, L1_xattn_mem_pool_norm_w, L1_xattn_to_mem_tokens_w, L1_xattn_ff_norm_w, L1_xattn_ff_w1, L1_xattn_ff_b1, L1_xattn_ff_w2, L1_xattn_ff_b2)
    return x

_drawn_inputs = setup_inputs


def setup_inputs(seed=0):
    import zlib

    import numpy as np

    out = dict(_drawn_inputs(seed))
    spreads = {'L0_xattn_bq': (0.0, 0.567),
     'L0_xattn_bk': (0.0, 0.8),
     'L0_xattn_bv': (0.0, 0.1),
     'L0_xattn_bo': (0.0, 0.1),
     'L0_xattn_gamma': (1.0, 0.2),
     'L0_xattn_beta': (0.0, 0.1),
     'L1_xattn_attn_norm_w': (1.0, 0.6),
     'L1_xattn_mem_pool_norm_w': (1.0, 0.6),
     'L1_xattn_ff_norm_w': (1.0, 0.6),
     'L1_xattn_ff_b1': (0.0, 0.8),
     'L1_xattn_ff_b2': (0.0, 0.1)}
    factors = {'L1_xattn_to_mem_tokens_w': 6.439, 'L1_xattn_ff_w1': 4.857, 'L1_xattn_ff_w2': 4.791}
    for name, (base, spread) in spreads.items():
        noise = np.random.default_rng([zlib.crc32(name.encode()), seed]).standard_normal(out[name].shape)
        drawn = base * np.exp(spread * noise) if base else spread * noise
        out[name] = jnp.asarray(drawn.astype(out[name].dtype))
    for name, factor in factors.items():
        out[name] = (out[name] * factor).astype(out[name].dtype)
    return out
```

```python
from contextlib import ExitStack

import numpy as np

import concourse.bass as bass
from concourse import mybir

ALU = mybir.AluOpType
ACT = mybir.ActivationFunctionType
F32 = mybir.dt.float32
BF16 = mybir.dt.bfloat16
AX_X = mybir.AxisListType.X

B, S, D = 64, 128, 128
S2 = 77
H = 16
HD0 = D // H
DH = 64
INNER = H * DH
PAIRS = H // 2
SEG = 64
NSEG = S // SEG
NPM, NM = 16, 16
PRE = 1 + NPM
KEYS = SEG + PRE
VW = DH + 1
PVN = 96
DFF = 341
FCH = 3
FROWS = [128, 128, DFF - 256]
LN_EPS, RMS_EPS = 1e-5, 1.1920929e-07
CLAMP = 50.0
BANK = 512
NEG = -1e30


def banks(ctx, nc, psum, stage, first_bank, n_banks, tasks):
    names = [t[0] for t in tasks]
    fills = [ctx.enter_context(nc.semaphore(f"{stage}_bank{first_bank + n}_filled")) for n in range(n_banks)]

    def at(task):
        return psum[:, first_bank + names.index(task) % n_banks, :]

    def fill(task):
        return fills[names.index(task) % n_banks]

    def is_filled(task, seq):
        n = names.index(task)
        uses = len(range(n % n_banks, len(names), n_banks))
        return fill(task), seq * uses + (n // n_banks + 1)

    def is_free(task, seq):
        n = names.index(task)
        if n >= n_banks:
            _, read, k, per_seq = tasks[n - n_banks]
            return read, seq * per_seq + k
        _, read, k, per_seq = tasks[max(range(n, len(names), n_banks))]
        return read, 0 if first(seq) else seq * per_seq + (k - per_seq)

    return at, fill, is_filled, is_free


def steps(semaphore, *names):
    return semaphore, lambda name, seq: seq * len(names) + (names.index(name) + 1)


def wait(eng, signal_count):
    signal, count = signal_count
    if not (isinstance(count, int) and count <= 0):
        eng.wait_ge(signal, count)


def passed(eng, signal):
    eng.sem_inc(signal, 1)


def first(seq):
    return isinstance(seq, int) and seq == 0


def build(nc, x, ctx_in, mask, Wq, bq, Wk, bk, Wv, bv, Wo, bo, gamma, beta, attn_norm_w, to_qkv_w,
          to_out_w, persist_mem, mem_pool_norm_w, to_mem_tokens_w, ff_norm_w, ff_w1, ff_b1, ff_w2, ff_b2,
          c_ident, c_rope, c_headmask, c_causal, c_shift, c_select, c_stack, out):
    with ExitStack() as ctx:
        def sb(name, shape, dt=F32):
            return ctx.enter_context(nc.sbuf_tensor(name, shape, dt))

        def sem(name):
            return ctx.enter_context(nc.semaphore(name))

        psum = ctx.enter_context(nc.psum_tensor("psum", [128, 8, BANK], F32))
        memv_dram = nc.dram_tensor("memv_dram", (B, INNER), F32, kind="Internal").ap()

        wq, wk, wv, wo = (sb(n, [D, D]) for n in ("wq", "wk", "wv", "wo"))
        wqkv = sb("wqkv", [D, 3 * INNER])
        wout = sb("wout", [128, PAIRS, D])
        wmem = sb("wmem", [D, D])
        w1 = sb("w1", [D, 2 * DFF])
        w2 = sb("w2", [128, FCH, D])
        cols = sb("cols", [128, 12])
        BQ, BK, NW, PW, FW = range(5)
        ff_bias = sb("ff_bias", [128, 2, FCH])
        neg_bg = sb("neg_bg", [128, FCH])
        bv_rep, bo_rep, ga_rep, be_rep, b2_rep = (sb(n, [128, D]) for n in ("bv_rep", "bo_rep", "ga_rep", "be_rep", "b2_rep"))
        ident = sb("ident", [128, 128])
        ident_b = sb("ident_b", [128, 128], BF16)
        rope = sb("rope", [128, 2, DH])
        headmask = sb("headmask", [128, H])
        causal_b = sb("causal_b", [128, SEG], BF16)
        select_b = sb("select_b", [128, H * NSEG, KEYS], BF16)
        stack_b = sb("stack_b", [128, SEG], BF16)
        shift_b = sb("shift_b", [128, SEG], BF16)

        x_sb = sb("x_sb", [S, D])
        ctx_sb = sb("ctx_sb", [S2, D])
        mask_sb = sb("mask_sb", [S, S2])
        xT = sb("xT", [D, S])
        ctxT = sb("ctxT", [D, S2])
        wT = sb("wT", [S2, S])
        xb = sb("xb", [S, D])
        q0T = sb("q0T", [D, S])
        kpad = sb("kpad", [D, H, S2])
        VB = 4 * HD0 + 40
        v0 = sb("v0", [S2, 4, 4, VB])
        z0 = sb("z0", [S2, H, S])
        rden0 = sb("rden0", [128, 2 * S])
        c0T = sb("c0T", [D, S])
        r0 = sb("r0", [S, D])
        t0 = sb("t0", [S, D])
        t0g = sb("t0g", [S, D])
        y = sb("y", [S, D])
        ysq = sb("ysq", [S, D])
        xn = sb("xn", [S, D])
        st0 = sb("st0", [S, 16])
        bn0 = sb("bn0", [S, 6])

        y_keep = sb("y_keep", [S, D])
        xnT = sb("xnT", [D, S])
        ra = sb("ra", [S, 2 * INNER])
        rb = sb("rb", [S, 2 * INNER])
        qpad = sb("qpad", [128, PAIRS, NSEG, 2, SEG])
        kall = sb("kall", [128, PAIRS, NSEG, KEYS])
        memk = sb("memk", [128, B, PAIRS])
        vall = [sb(f"vall{s}", [KEYS, H * VW + PVN - VW]) for s in range(NSEG)]
        mx = sb("mx", [S, H])
        mt = sb("mt", [S, NSEG, 2, H], BF16)
        probs = sb("probs", [KEYS, PAIRS, NSEG, 2, SEG])
        rden1 = sb("rden1", [S, H])
        o = sb("o", [S, H, DH])
        oT = sb("oT", [128, PAIRS, S])
        x1 = sb("x1", [S, D])
        x1sq = sb("x1sq", [S, D])
        hn = sb("hn", [S, D])
        st1 = sb("st1", [S, 8])

        hnT = sb("hnT", [D, S])
        eg = sb("eg", [128, FCH, S])
        ug = sb("ug", [128, FCH, S])
        sT = sb("sT", [128, FCH, S])
        x1b = sb("x1b", [S, D])
        out_sb = sb("out_sb", [S, D])

        ctx_all = sb("ctx_all", [S2, B, D])
        stage = sb("stage", [128, H * NSEG * KEYS])
        stage2 = sb("stage2", [128, 3 * SEG])
        ones = sb("ones", [S2, 1])
        nhalf = sb("nhalf", [128, 1])
        pm_sb = sb("pm_sb", [NPM, INNER])
        pool_T = sb("pool_T", [D, B])
        pool_n = sb("pool_n", [B, 3, D])
        pool_st = sb("pool_st", [B, 4])
        pool_nT = sb("pool_nT", [D, B])
        memT = sb("memT", [D, B])
        memv = sb("memv", [B, INNER])

        w_in = sem("w_in")
        ctx_all_in = sem("ctx_all_in")
        pm_v_in = sem("pm_v_in")
        zeros_step = sem("zeros_step")
        zeros_set = sem("zeros_set")
        consts_cast = sem("consts_cast")
        setup_pe, setup_act, setup_dve, setup_pool = sem("setup_pe"), sem("setup_act"), sem("setup_dve"), sem("setup_pool")
        memv_stored = sem("memv_stored")
        dve_passed, pool_passed, sp_passed = sem("dve_passed"), sem("pool_passed"), sem("sp_passed")
        x_in, ctx_loaded, mask_in = sem("x_in"), sem("ctx_loaded"), sem("mask_in")
        inT_ready = sem("inT_ready")
        xb_ready = sem("xb_ready")
        qkv0_ready = sem("qkv0_ready")
        z_ready = sem("z_ready")
        clip_ready = sem("clip_ready")
        exp0_ready = sem("exp0_ready")
        c0T_ready = sem("c0T_ready")
        var0_ready, rstd0_ready = sem("var0_ready"), sem("rstd0_ready")
        ms0_ready, rms0_ready = sem("ms0_ready"), sem("rms0_ready")
        ms1_ready, rms1_ready = sem("ms1_ready"), sem("rms1_ready")
        xn_ready = sem("xn_ready")
        cross_step = sem("cross_step")
        ykeep_ready = sem("ykeep_ready")
        xnT_ready = sem("xnT_ready")
        rope_ready = sem("rope_ready")
        rot_ready = sem("rot_ready")
        qk_ready = sem("qk_ready")
        memk_ready = sem("memk_ready")
        memv_in = sem("memv_in")
        v_ready = sem("v_ready")
        max_ready = sem("max_ready")
        mt_ready = sem("mt_ready")
        shift_ready = sem("shift_ready")
        probs_ready = sem("probs_ready")
        o_ready = sem("o_ready")
        oT_ready = sem("oT_ready")
        x1_ready = sem("x1_ready")
        hn_ready = sem("hn_ready")
        self_step = sem("self_step")
        hnT_ready = sem("hnT_ready")
        x1b_ready = sem("x1b_ready")
        eg_ready = sem("eg_ready")
        sT_ready = sem("sT_ready")
        ff_step = sem("ff_step")
        out_ready = sem("out_ready")
        out_stored = sem("out_stored")

        cross_at, cross_fill, cross_filled, cross_free = banks(ctx, nc, psum, "cross", 0, 3, [
            ("inT", inT_ready, 1, 1), ("qkv", qkv0_ready, 1, 1), *[(f"score{t}", z_ready, t + 1, 4) for t in range(4)],
            ("pv", c0T_ready, 1, 1), ("wo", xn_ready, 1, 1)])
        self_at, self_fill, self_filled, self_free = banks(ctx, nc, psum, "self", 3, 3, [
            ("xnT", xnT_ready, 1, 1), *[(f"qkv{t}", rope_ready, t + 1, 4) for t in range(4)],
            *[(f"qkv{4 + t}", v_ready, t + 1, 2) for t in range(2)], *[(f"qkT{t}", qk_ready, t + 1, 4) for t in range(4)],
            *[(f"max{t}", max_ready, t + 1, 4) for t in range(4)], ("shift", shift_ready, 1, 1),
            *[(f"score{t}", probs_ready, t + 1, 4) for t in range(4)], *[(f"pv{t}", o_ready, t + 1, 4) for t in range(4)],
            *[(f"oT{t}", oT_ready, t + 1, 2) for t in range(2)], ("out", x1_ready, 1, 1)])
        ff_at, ff_fill, ff_filled, ff_free = banks(ctx, nc, psum, "ff", 6, 2, [
            ("hnT", hnT_ready, 1, 1), ("gate", sT_ready, 1, 1), ("lin", sT_ready, 1, 1), ("down", out_ready, 1, 1)])
        cross_steps = steps(cross_step, "rden", "r", "bn", "mean", "norm", "gamma", "y", "square")
        self_steps = steps(self_step, "hi", *[f"rden{t}" for t in range(4)], "square")
        ff_steps = steps(ff_step, "plus1", "sigmoid", "silu")

        weight_loads = [
            (wq[:], Wq), (wk[:], Wk), (wv[:], Wv), (wo[:], Wo), (wqkv[:], to_qkv_w),
            (wout[:], to_out_w.rearrange("(c p) n -> p c n", p=128)), (wmem[:], to_mem_tokens_w), (w1[:], ff_w1),
            (w2[:, 0:2, :], ff_w2[0:256, :].rearrange("(c p) n -> p c n", p=128)), (w2[0:FROWS[2], 2, :], ff_w2[256:DFF, :]),
            (ident[:], c_ident), (rope[:], c_rope), (headmask[:], c_headmask),
            (stage2[:, 0:SEG], c_causal), (stage2[:, SEG:2 * SEG], c_stack), (stage2[:, 2 * SEG:3 * SEG], c_shift),
            (stage[:], c_select), (pm_sb[:].rearrange("n (h d) -> n h d", h=H), persist_mem.rearrange("h n d -> n h d")),
        ]
        weight_loads += [(cols[:, n:n + 1], v.rearrange("(p a) -> p a", a=1))
                         for n, v in ((BQ, bq), (BK, bk), (NW, attn_norm_w), (PW, mem_pool_norm_w), (FW, ff_norm_w))]
        for part in range(2):
            for c in range(FCH):
                lo = part * DFF + 128 * c
                weight_loads.append((ff_bias[0:FROWS[c], part, c:c + 1],
                                     ff_b1[lo:lo + FROWS[c]].rearrange("(p a) -> p a", a=1)))
        weight_loads += [(t[:], v.rearrange("(a n) -> a n", a=1).broadcast_to([128, D]))
                         for t, v in ((bv_rep, bv), (bo_rep, bo), (ga_rep, gamma), (be_rep, beta), (b2_rep, ff_b2))]
        WEIGHTS_IN = 16 * len(weight_loads)

        block = ctx.enter_context(nc.Block())

        def pipeline(eng, body):
            body(0, None, None)
            body(1, 0, None)
            body(2, 1, 0)
            with eng.Fori(1, B - 2) as i:
                body(i + 2, i + 1, i)
            body(None, B - 1, B - 2)
            body(None, None, B - 1)

        @block.sync
        def _(sp):
            sp.dma_start(ctx_all[:], ctx_in.rearrange("b s d -> s b d")).then_inc(ctx_all_in, 16)
            for dst, src in weight_loads:
                sp.dma_start(dst, src).then_inc(w_in, 16)
            sp.wait_ge(zeros_set, 2)
            for s in range(NSEG):
                sp.dma_start(vall[s][SEG + 1:KEYS, 0:H * VW].rearrange("n (h w) -> n h w", h=H)[:, :, 0:DH],
                             persist_mem.rearrange("h n d -> n h d")).then_inc(pm_v_in, 16)
            sp.wait_ge(setup_act, 7)
            sp.dma_start(memv_dram, memv[:]).then_inc(memv_stored, 16)
            sp.wait_ge(memv_stored, 16)

            def body(c, a, f):
                if c is not None:
                    if not first(c):
                        wait(sp, cross_filled("inT", c - 1))
                        passed(sp, sp_passed)
                    wait(sp, (xb_ready, c))
                    passed(sp, sp_passed)
                    sp.dma_start(x_sb[:], x[bass.ds(c, 1), :, :].rearrange("b s d -> (b s) d")).then_inc(x_in, 16)
                    sp.dma_start(ctx_sb[:], ctx_in[bass.ds(c, 1), :, :].rearrange("b s d -> (b s) d")).then_inc(ctx_loaded, 16)
                    sp.dma_start(mask_sb[:], mask[bass.ds(c, 1), :, :, :].rearrange("b u s k -> (b u s) k")).then_inc(mask_in, 16)
                if a is not None:
                    if not first(a):
                        wait(sp, self_filled("pv3", a - 1))
                        passed(sp, sp_passed)
                    for s in range(NSEG):
                        sp.dma_start(vall[s][SEG:SEG + 1, 0:H * VW].rearrange("n (h w) -> n h w", h=H)[:, :, 0:DH],
                                     memv_dram[bass.ds(a, 1), :].rearrange("b (h d) -> b h d", h=H)).then_inc(memv_in, 16)
                if f is not None:
                    sp.wait_ge(out_ready, f + 1)
                    passed(sp, sp_passed)
                    sp.dma_start(out[bass.ds(f, 1), :, :].rearrange("b s d -> (b s) d"), out_sb[:]).then_inc(out_stored, 16)

            pipeline(sp, body)
            sp.wait_ge(out_stored, 16 * B)

        @block.gpsimd
        def _(pool):
            for t in (*vall, qpad, kpad, v0, mt, eg):
                nc.gpsimd.memset(t[:], 0.0).then_inc(zeros_step, 1)
            pool.wait_ge(zeros_step, 7)
            nc.gpsimd.memset(ones[:], 1.0)
            nc.gpsimd.memset(nhalf[:], -0.5)
            nc.gpsimd.memset(v0[:, :, :, 4 * HD0:5 * HD0], 1.0)
            for s in range(NSEG):
                nc.gpsimd.memset(vall[s][:, 0:H * VW].rearrange("n (h w) -> n h w", h=H)[:, :, DH:VW], 1.0).then_inc(zeros_step, 1)
            pool.wait_ge(zeros_step, 9)
            for s in range(NSEG):
                mem_col = vall[s][SEG:SEG + 1, 0:H * VW].rearrange("n (h w) -> n h w", h=H)[:, :, DH:VW]
                nc.gpsimd.memset(mem_col, float(NM)).then_inc(zeros_set, 1)
            pool.wait_ge(w_in, WEIGHTS_IN)
            pool.wait_ge(setup_dve, 3)
            nc.gpsimd.tensor_tensor(pool_st[:, 2:3], pool_st[:, 1:2], nhalf[0:B, :], ALU.pow).then_inc(setup_pool, 1)
            pool.wait_ge(setup_act, 7)

            def body(c, a, f):
                if f is not None:
                    pool.wait_ge(x1_ready, f + 1)
                    wait(pool, (out_ready, f))
                    nc.gpsimd.tensor_tensor(x1b[:], x1[:], b2_rep[:], ALU.add).then_inc(x1b_ready, 1)
                if a is not None:
                    pool.wait_ge(xn_ready, a + 1)
                    wait(pool, (x1_ready, a))
                    passed(pool, pool_passed)
                    nc.gpsimd.tensor_scalar(y_keep[:], y[:], 1.0, 0.0, ALU.mult, ALU.add).then_inc(ykeep_ready, 1)
                if c is not None:
                    pool.wait_ge(x_in, (c + 1) * 16)
                    wait(pool, (xn_ready, c))
                    nc.gpsimd.tensor_tensor(xb[:], x_sb[:], bo_rep[:], ALU.add).then_inc(xb_ready, 1)
                if a is not None:
                    if not first(a):
                        wait(pool, self_filled("score3", a - 1))
                    mk = memk[:, bass.ds(a, 1), :].rearrange("p b c -> p c b").unsqueeze(2).broadcast_to([128, PAIRS, NSEG, 1])
                    nc.gpsimd.tensor_copy(kall[:, :, :, SEG:SEG + 1], mk).then_inc(memk_ready, 1)
                    for t in range(4):
                        pool.wait_ge(rope_ready, a * 4 + (t + 1))
                        sl = slice(BANK * t, BANK * (t + 1))
                        nc.gpsimd.tensor_tensor(ra[:, sl], ra[:, sl], rb[:, sl], ALU.add).then_inc(rot_ready, 1)
                if c is not None:
                    lim = CLAMP * float(HD0) ** 0.5
                    for t in range(4):
                        pool.wait_ge(z_ready, c * 4 + (t + 1))
                        passed(pool, pool_passed)
                        zt = z0[:, 4 * t:4 * t + 4, :]
                        nc.gpsimd.tensor_scalar(zt, zt, lim, -lim, ALU.min, ALU.max).then_inc(clip_ready, 1)
                    pool.wait_ge(var0_ready, c + 1)
                    nc.gpsimd.tensor_tensor(st0[:, 3:4], st0[:, 2:3], nhalf[:], ALU.pow).then_inc(rstd0_ready, 1)
                    pool.wait_ge(ms0_ready, c + 1)
                    nc.gpsimd.tensor_tensor(st0[:, 6:7], st0[:, 5:6], nhalf[:], ALU.pow).then_inc(rms0_ready, 1)
                if a is not None:
                    pool.wait_ge(ms1_ready, a + 1)
                    nc.gpsimd.tensor_tensor(st1[:, 2:3], st1[:, 1:2], nhalf[:], ALU.pow).then_inc(rms1_ready, 1)

            pipeline(pool, body)

        @block.scalar
        def _(act):
            copy = lambda out, in_, **k: nc.scalar.activation(out, in_, ACT.Copy, **k)
            bank = lambda n: psum[:, n, :]
            act.wait_ge(w_in, WEIGHTS_IN)
            for n in range(FCH):
                nc.scalar.mul(neg_bg[0:FROWS[n], n:n + 1], ff_bias[0:FROWS[n], 1, n:n + 1], -1.0)
            act.wait_ge(setup_pe, 1)
            copy(pool_T[:], bank(0)[:, 0:B], scale=1.0 / S2).then_inc(setup_act, 1)
            act.wait_ge(setup_pe, 3)
            copy(pool_nT[:], bank(2)[:, 0:B], scale=cols[:, PW:PW + 1]).then_inc(setup_act, 1)
            act.wait_ge(setup_pe, 4)
            copy(memT[:], bank(3)[:, 0:B]).then_inc(setup_act, 1)
            act.wait_ge(setup_pe, 5)
            copy(memk[:].rearrange("p b c -> p c b"), bank(4).rearrange("p (c b) -> p c b", c=PAIRS)).then_inc(setup_act, 1)
            for t in range(2):
                copy(memv[:, BANK * t:BANK * (t + 1)], bank(5 + t)[0:B, :], scale=float(NM)).then_inc(setup_act, 1)
            pk = bank(7)[:, 0:PAIRS * NPM].rearrange("p (c n) -> p c n", c=PAIRS)
            for s in range(NSEG):
                last = copy(kall[:, :, s, SEG + 1:KEYS], pk)
            last.then_inc(setup_act, 1)
            act.wait_ge(zeros_set, 2)

            def body(c, a, f):
                if c is not None:
                    wait(act, cross_filled("inT", c))
                    wait(act, (z_ready, c * 4))
                    p = cross_at("inT")
                    copy(xT[:], p[:, 0:S])
                    copy(ctxT[:], p[:, S:S + S2])
                    copy(wT[:], p[0:S2, 256:256 + S], scale=0.5, bias=0.5).then_inc(inT_ready, 1)
                if a is not None:
                    wait(act, self_filled("xnT", a))
                    copy(xnT[:], self_at("xnT")[:, 0:S], scale=cols[:, NW:NW + 1]).then_inc(xnT_ready, 1)
                if f is not None:
                    wait(act, ff_filled("hnT", f))
                    copy(hnT[:], ff_at("hnT")[:, 0:S], scale=cols[:, FW:FW + 1]).then_inc(hnT_ready, 1)
                if a is not None:
                    for t in range(2):
                        wait(act, self_filled(f"qkv{4 + t}", a))
                        for s in range(NSEG):
                            dst = vall[s][0:SEG, VW * 8 * t:VW * 8 * (t + 1)].rearrange("n (h w) -> n h w", h=8)[:, :, 0:DH]
                            last = copy(dst, self_at(f"qkv{4 + t}")[SEG * s:SEG * (s + 1), :].rearrange("n (h d) -> n h d", h=8))
                        last.then_inc(v_ready, 1)
                if f is not None:
                    wait(act, ff_filled("gate", f))
                    for n in range(FCH):
                        m = FROWS[n]
                        last = nc.scalar.activation(eg[0:m, n, :], ff_at("gate")[0:m, S * n:S * (n + 1)], ACT.Exp,
                                                    scale=-1.0, bias=neg_bg[0:m, n:n + 1])
                    last.then_inc(eg_ready, 1)
                if c is not None:
                    for t in range(4):
                        act.wait_ge(clip_ready, c * 4 + (t + 1))
                        zt = z0[:, 4 * t:4 * t + 4, :]
                        nc.scalar.activation(zt, zt, ACT.Exp, scale=float(HD0) ** -0.5).then_inc(exp0_ready, 1)
                if a is not None:
                    for t in range(2):
                        wait(act, self_filled(f"qkT{t}", a))
                        for h in range(2):
                            rows = slice(DH * h, DH * (h + 1))
                            last = copy(qpad[rows, 4 * t:4 * t + 4, :, h, :],
                                        self_at(f"qkT{t}")[rows, :].rearrange("p (c s i) -> p c s i", c=4, s=NSEG))
                        last.then_inc(qk_ready, 1)
                    for t in range(2):
                        wait(act, self_filled(f"qkT{2 + t}", a))
                        copy(kall[:, 4 * t:4 * t + 4, :, 0:SEG],
                             self_at(f"qkT{2 + t}").rearrange("p (c s j) -> p c s j", c=4, s=NSEG)).then_inc(qk_ready, 1)
                    for t in range(4):
                        wait(act, self_filled(f"score{t}", a))
                        nc.scalar.activation(probs[:, 2 * t:2 * t + 2, :, :, :].rearrange("k c s h i -> k (c s h i)"),
                                             self_at(f"score{t}")[0:KEYS, :], ACT.Exp, scale=float(DH) ** -0.5).then_inc(probs_ready, 1)
                    for t in range(2):
                        wait(act, self_filled(f"oT{t}", a))
                        copy(oT[:, 4 * t:4 * t + 4, :].rearrange("p c s -> p (c s)"), self_at(f"oT{t}")).then_inc(oT_ready, 1)

            pipeline(act, body)

        @block.vector
        def _(dve):
            V = nc.vector

            def then(ins, steps_of, name, seq):
                semaphore, done = steps_of
                ins.then_inc(semaphore, 1)
                wait(dve, (semaphore, done(name, seq)))

            dve.wait_ge(w_in, WEIGHTS_IN)
            V.tensor_copy(ident_b[:], ident[:])
            V.tensor_copy(causal_b[:], stage2[:, 0:SEG])
            V.tensor_copy(stack_b[:], stage2[:, SEG:2 * SEG])
            V.tensor_copy(shift_b[:], stage2[:, 2 * SEG:3 * SEG])
            V.tensor_copy(select_b[:].rearrange("p n k -> p (n k)"), stage[:]).then_inc(consts_cast, 1)
            dve.wait_ge(setup_pe, 2)
            V.tensor_copy(pool_n[:, 0, :], psum[0:B, 1, 0:D]).then_inc(setup_dve, 1)
            dve.wait_ge(setup_dve, 1)
            V.tensor_tensor_reduce(out=pool_n[:, 1, :], in0=pool_n[:, 0, :], in1=pool_n[:, 0, :], scale=1.0, scalar=0.0,
                                   op0=ALU.mult, op1=ALU.add, accum_out=pool_st[:, 0:1]).then_inc(setup_dve, 1)
            dve.wait_ge(setup_dve, 2)
            V.tensor_scalar(pool_st[:, 1:2], pool_st[:, 0:1], 1.0 / D, RMS_EPS, ALU.mult, ALU.add).then_inc(setup_dve, 1)
            dve.wait_ge(setup_pool, 1)
            V.tensor_scalar(pool_n[:, 2, :], pool_n[:, 0, :], pool_st[:, 2:3], None, ALU.mult).then_inc(setup_dve, 1)
            dve.wait_ge(zeros_set, 2)

            def body(c, a, f):
                if c is not None:
                    wait(dve, cross_filled("qkv", c))
                    p = cross_at("qkv")
                    V.tensor_scalar(q0T[:], p[:, 0:S], cols[:, BQ:BQ + 1], None, ALU.add)
                    V.scalar_tensor_tensor(out=kpad[:], in0=p[:, S:S + S2].unsqueeze(1).broadcast_to([D, H, S2]),
                                           scalar=cols[:, BK:BK + 1], in1=headmask[:].unsqueeze(2).broadcast_to([D, H, S2]),
                                           op0=ALU.add, op1=ALU.mult)
                    V.tensor_tensor(v0[:, :, :, 0:HD0], p[0:S2, 256:384].rearrange("k (g r d) -> k g r d", g=4, r=4),
                                    bv_rep[0:S2, :].rearrange("k (g r d) -> k g r d", g=4, r=4), ALU.add).then_inc(qkv0_ready, 1)
                if a is not None:
                    for t in range(4):
                        wait(dve, self_filled(f"qkv{t}", a))
                        p = self_at(f"qkv{t}").rearrange("n (h d) -> n h d", h=8)
                        sl = slice(BANK * t, BANK * (t + 1))
                        V.tensor_tensor(ra[:, sl].rearrange("n (h d) -> n h d", h=8), p,
                                        rope[:, 0, :].unsqueeze(1).broadcast_to([S, 8, DH]), ALU.mult)
                        p = self_at(f"qkv{t}").rearrange("n (h e t) -> n h e t", h=8, t=2)[:, :, :, ::-1]
                        V.tensor_tensor(rb[:, sl].rearrange("n (h e t) -> n h e t", h=8, t=2), p,
                                        rope[:, 1, :].rearrange("n (e t) -> n e t", t=2).unsqueeze(1).broadcast_to([S, 8, DH // 2, 2]),
                                        ALU.mult).then_inc(rope_ready, 1)
                if f is not None:
                    dve.wait_ge(eg_ready, f + 1)
                    then(V.tensor_scalar(ug[:], eg[:], 1.0, None, ALU.add), ff_steps, "plus1", f)
                    then(V.reciprocal(ug[:], ug[:]), ff_steps, "sigmoid", f)
                    for n in range(FCH):
                        m = FROWS[n]
                        last = V.scalar_tensor_tensor(out=ug[0:m, n, :], in0=ff_at("gate")[0:m, S * n:S * (n + 1)],
                                                      scalar=ff_bias[0:m, 1, n:n + 1], in1=ug[0:m, n, :], op0=ALU.add, op1=ALU.mult)
                    then(last, ff_steps, "silu", f)
                    wait(dve, ff_filled("lin", f))
                    for n in range(FCH):
                        m = FROWS[n]
                        last = V.scalar_tensor_tensor(out=sT[0:m, n, :], in0=ff_at("lin")[0:m, S * n:S * (n + 1)],
                                                      scalar=ff_bias[0:m, 0, n:n + 1], in1=ug[0:m, n, :], op0=ALU.add, op1=ALU.mult)
                    last.then_inc(sT_ready, 1)
                if c is not None:
                    dve.wait_ge(inT_ready, c + 1)
                    for t in range(4):
                        wait(dve, cross_filled(f"score{t}", c))
                        V.tensor_tensor(z0[:, 4 * t:4 * t + 4, :], cross_at(f"score{t}")[0:S2, :].rearrange("k (h q) -> k h q", h=4),
                                        wT[:].unsqueeze(1).broadcast_to([S2, 4, S]), ALU.mult).then_inc(z_ready, 1)
                if f is not None:
                    wait(dve, ff_filled("down", f))
                    dve.wait_ge(x1b_ready, f + 1)
                    wait(dve, (out_stored, f * 16))
                    V.tensor_tensor(out_sb[:], ff_at("down")[:, 0:D], x1b[:], ALU.add).then_inc(out_ready, 1)
                if a is not None:
                    for t in range(4):
                        wait(dve, self_filled(f"max{t}", a))
                        V.reduce_max(mx[:, 4 * t:4 * t + 4], self_at(f"max{t}")[:, 0:4 * KEYS].rearrange("n (h k) -> n h k", h=4),
                                     AX_X).then_inc(max_ready, 1)
                    dve.wait_ge(max_ready, a * 4 + 4)
                    for s in range(NSEG):
                        rows = slice(SEG * s, SEG * (s + 1))
                        last = V.tensor_scalar(mt[rows, s, 0, :], mx[rows, :], -1.0, None, ALU.mult)
                    then(last, self_steps, "hi", a)
                    for s in range(NSEG):
                        rows = slice(SEG * s, SEG * (s + 1))
                        last = V.scalar_tensor_tensor(out=mt[rows, s, 1, :], in0=mx[rows, :], scalar=-1.0, in1=mt[rows, s, 0, :],
                                                      op0=ALU.mult, op1=ALU.subtract)
                    last.then_inc(mt_ready, 1)
                    wait(dve, self_filled("shift", a))
                    V.tensor_copy(shift_b[0:64, :], self_at("shift")[0:64, 0:SEG]).then_inc(shift_ready, 1)
                if c is not None:
                    wait(dve, cross_filled("pv", c))
                    p = cross_at("pv")
                    for half in (0, 64):
                        last = V.reciprocal(rden0[half:half + 32, :], p[half + 32:half + 64, 0:2 * S])
                    then(last, cross_steps, "rden", c)
                    for g in range(4):
                        half, q = 64 * (g % 2), slice(S * (g // 2), S * (g // 2 + 1))
                        last = V.tensor_tensor(c0T[32 * g:32 * g + 32, :], p[half:half + 32, q], rden0[half:half + 32, q], ALU.mult)
                    last.then_inc(c0T_ready, 1)
                    wait(dve, cross_filled("wo", c))
                    dve.wait_ge(xb_ready, c + 1)
                    then(V.tensor_tensor(r0[:], cross_at("wo")[:, 0:D], xb[:], ALU.add), cross_steps, "r", c)
                    V.bn_stats(bn0[:], r0[:]).then_inc(cross_step, 1)
                    wait(dve, (cross_step, cross_steps[1]("bn", c)))
                    passed(dve, dve_passed)
                    then(V.bn_aggr(st0[:, 0:2], bn0[:]), cross_steps, "mean", c)
                    V.tensor_scalar(st0[:, 2:3], st0[:, 1:2], LN_EPS, None, ALU.add).then_inc(var0_ready, 1)
                    dve.wait_ge(rstd0_ready, c + 1)
                    then(V.tensor_scalar(t0[:], r0[:], st0[:, 0:1], st0[:, 3:4], ALU.subtract, ALU.mult), cross_steps, "norm", c)
                    then(V.tensor_tensor(t0g[:], t0[:], ga_rep[:], ALU.mult), cross_steps, "gamma", c)
                    wait(dve, (ykeep_ready, c))
                    then(V.tensor_tensor(y[:], t0g[:], be_rep[:], ALU.add), cross_steps, "y", c)
                    then(V.tensor_tensor_reduce(out=ysq[:], in0=y[:], in1=y[:], scale=1.0, scalar=0.0, op0=ALU.mult, op1=ALU.add,
                                                accum_out=st0[:, 4:5]), cross_steps, "square", c)
                    V.tensor_scalar(st0[:, 5:6], st0[:, 4:5], 1.0 / D, RMS_EPS, ALU.mult, ALU.add).then_inc(ms0_ready, 1)
                    if not first(c):
                        wait(dve, self_filled("xnT", c - 1))
                    dve.wait_ge(rms0_ready, c + 1)
                    V.tensor_scalar(xn[:], y[:], st0[:, 6:7], None, ALU.mult).then_inc(xn_ready, 1)
                if a is not None:
                    for t in range(4):
                        wait(dve, self_filled(f"pv{t}", a))
                        p = self_at(f"pv{t}")[:, 0:4 * PVN].rearrange("n (h w) -> n h w", h=4)
                        then(V.reciprocal(rden1[:, 4 * t:4 * t + 4].unsqueeze(2), p[:, :, DH:VW]), self_steps, f"rden{t}", a)
                        V.tensor_tensor(o[:, 4 * t:4 * t + 4, :], p[:, :, 0:DH],
                                        rden1[:, 4 * t:4 * t + 4].unsqueeze(2).broadcast_to([S, 4, DH]), ALU.mult).then_inc(o_ready, 1)
                    wait(dve, self_filled("out", a))
                    dve.wait_ge(ykeep_ready, a + 1)
                    wait(dve, (x1b_ready, a))
                    V.tensor_tensor(x1[:], self_at("out")[:, 0:D], y_keep[:], ALU.add).then_inc(x1_ready, 1)
                    dve.wait_ge(x1_ready, a + 1)
                    then(V.tensor_tensor_reduce(out=x1sq[:], in0=x1[:], in1=x1[:], scale=1.0, scalar=0.0, op0=ALU.mult, op1=ALU.add,
                                                accum_out=st1[:, 0:1]), self_steps, "square", a)
                    V.tensor_scalar(st1[:, 1:2], st1[:, 0:1], 1.0 / D, RMS_EPS, ALU.mult, ALU.add).then_inc(ms1_ready, 1)
                    if not first(a):
                        wait(dve, ff_filled("hnT", a - 1))
                    dve.wait_ge(rms1_ready, a + 1)
                    V.tensor_scalar(hn[:], x1[:], st1[:, 2:3], None, ALU.mult).then_inc(hn_ready, 1)

            pipeline(dve, body)

        @block.tensor
        def _(pe):
            def mm(o, l, r, start=True, stop=True):
                return nc.tensor.matmul(o, l, r, start=start, stop=stop, skip_group_check=True)

            bank = lambda n: psum[:, n, :]
            pe.wait_ge(ctx_all_in, 16)
            pe.wait_ge(zeros_set, 2)
            for b in range(B):
                last = mm(bank(0)[:, b:b + 1], ctx_all[:, b, :], ones[:])
            last.then_inc(setup_pe, 1)
            pe.wait_ge(w_in, WEIGHTS_IN)
            pe.wait_ge(setup_act, 1)
            nc.tensor.transpose(bank(1)[0:B, 0:D], pool_T[:], ident[:]).then_inc(setup_pe, 1)
            pe.wait_ge(setup_dve, 4)
            nc.tensor.transpose(bank(2)[:, 0:B], pool_n[:, 2, :], ident[0:B, 0:B]).then_inc(setup_pe, 1)
            pe.wait_ge(setup_act, 2)
            mm(bank(3)[:, 0:B], wmem[:], pool_nT[:]).then_inc(setup_pe, 1)
            pe.wait_ge(setup_act, 3)
            for n in range(PAIRS):
                mm(bank(4)[:, B * n:B * (n + 1)], wqkv[:, INNER + 128 * n:INNER + 128 * (n + 1)], memT[:])
            for t in range(2):
                mm(bank(5 + t)[0:B, :], memT[:], wqkv[:, 2 * INNER + BANK * t:2 * INNER + BANK * (t + 1)])
            for n in range(PAIRS):
                last = nc.tensor.transpose(bank(7)[:, NPM * n:NPM * (n + 1)], pm_sb[:, 128 * n:128 * (n + 1)], ident[0:NPM, 0:NPM])
            last.then_inc(setup_pe, 1)
            pe.wait_ge(setup_act, 7)
            pe.wait_ge(consts_cast, 1)
            pe.wait_ge(pm_v_in, 16 * NSEG)

            q_hi = qpad[:].bitcast(BF16).rearrange("p c s h (i t) -> p c s h i t", t=2)[:, :, :, :, :, 1]
            k_hi = kall[:].bitcast(BF16).rearrange("p c s (k t) -> p c s k t", t=2)[:, :, :, :, 1]
            v0_flat = v0[:].rearrange("k g r w -> k (g r w)")

            def body(c, a, f):
                if c is not None:
                    wait(pe, cross_free("inT", c))
                    pe.wait_ge(x_in, (c + 1) * 16)
                    pe.wait_ge(ctx_loaded, (c + 1) * 16)
                    pe.wait_ge(mask_in, (c + 1) * 16)
                    p = cross_at("inT")
                    nc.tensor.transpose(p[:, 0:S], x_sb[:], ident[:])
                    nc.tensor.transpose(p[:, S:S + S2], ctx_sb[:], ident[0:S2, 0:S2])
                    nc.tensor.transpose(p[0:S2, 256:256 + S], mask_sb[:], ident[:]).then_inc(cross_fill("inT"), 1)
                if a is not None:
                    wait(pe, self_free("xnT", a))
                    pe.wait_ge(xn_ready, a + 1)
                    nc.tensor.transpose(self_at("xnT")[:, 0:S], xn[:], ident[:]).then_inc(self_fill("xnT"), 1)
                if f is not None:
                    wait(pe, ff_free("hnT", f))
                    pe.wait_ge(hn_ready, f + 1)
                    nc.tensor.transpose(ff_at("hnT")[:, 0:S], hn[:], ident[:]).then_inc(ff_fill("hnT"), 1)
                if c is not None:
                    wait(pe, cross_free("qkv", c))
                    pe.wait_ge(inT_ready, c + 1)
                    p = cross_at("qkv")
                    mm(p[:, 0:S], wq[:], xT[:])
                    mm(p[:, S:S + S2], wk[:], ctxT[:])
                    mm(p[0:S2, 256:256 + D], ctxT[:], wv[:]).then_inc(cross_fill("qkv"), 1)
                if a is not None:
                    pe.wait_ge(xnT_ready, a + 1)
                    for t in range(6):
                        wait(pe, self_free(f"qkv{t}", a))
                        mm(self_at(f"qkv{t}"), xnT[:], wqkv[:, BANK * t:BANK * (t + 1)]).then_inc(self_fill(f"qkv{t}"), 1)
                if f is not None:
                    pe.wait_ge(hnT_ready, f + 1)
                    for name, part in (("gate", 1), ("lin", 0)):
                        wait(pe, ff_free(name, f))
                        for n in range(FCH):
                            lo = DFF * part + 128 * n
                            last = mm(ff_at(name)[0:FROWS[n], S * n:S * (n + 1)], w1[:, lo:lo + FROWS[n]], hnT[:])
                        last.then_inc(ff_fill(name), 1)
                if c is not None:
                    pe.wait_ge(qkv0_ready, c + 1)
                    for t in range(4):
                        wait(pe, cross_free(f"score{t}", c))
                        for n in range(4):
                            last = mm(cross_at(f"score{t}")[0:S2, S * n:S * (n + 1)], kpad[:, 4 * t + n, :], q0T[:])
                        last.then_inc(cross_fill(f"score{t}"), 1)
                if f is not None:
                    pe.wait_ge(sT_ready, f + 1)
                    for n in range(FCH):
                        m = FROWS[n]
                        last = mm(ff_at("down")[:, 0:D], sT[0:m, n, :], w2[0:m, n, :], start=n == 0, stop=n == FCH - 1)
                    last.then_inc(ff_fill("down"), 1)
                if a is not None:
                    for t in range(4):
                        wait(pe, self_free(f"qkT{t}", a))
                        pe.wait_ge(rot_ready, a * 4 + (t + 1))
                        for n in range(4):
                            last = nc.tensor.transpose(self_at(f"qkT{t}")[:, 128 * n:128 * (n + 1)],
                                                       ra[:, BANK * t + 128 * n:BANK * t + 128 * (n + 1)], ident[:])
                        last.then_inc(self_fill(f"qkT{t}"), 1)
                    pe.wait_ge(qk_ready, a * 4 + 4)
                    pe.wait_ge(memk_ready, a + 1)
                    for t in range(4):
                        if t == 3:
                            wait(pe, self_free(f"max{t}", a))
                        p = self_at(f"max{t}")[:, 0:4 * KEYS].rearrange("n (h k) -> n h k", h=4)
                        mm(p[:, :, 0:SEG], ident_b[:], causal_b[:].unsqueeze(1).broadcast_to([128, 4, SEG]), stop=False)
                        for n in range(4):
                            pair, h = 2 * t + n // 2, n % 2
                            for s in range(NSEG):
                                last = mm(p[SEG * s:SEG * (s + 1), n, :], q_hi[:, pair, s, h, :], k_hi[:, pair, s, :], start=False)
                        last.then_inc(self_fill(f"max{t}"), 1)
                if c is not None:
                    wait(pe, cross_free("pv", c))
                    for g in range(4):
                        if g % 2 == 0:
                            pe.wait_ge(exp0_ready, c * 4 + (g + 2))
                            for r in range(4):
                                for gg in (g, g + 1):
                                    half, q = 64 * (gg % 2), slice(S * (gg // 2), S * (gg // 2 + 1))
                                    last = mm(cross_at("pv")[half:half + 64, q], v0_flat[:, 4 * VB * gg + 64 * r:4 * VB * gg + 64 * r + 64],
                                              z0[:, 4 * gg + r, :], start=r == 0, stop=r == 3)
                    last.then_inc(cross_fill("pv"), 1)
                if a is not None:
                    wait(pe, self_free("shift", a))
                    pe.wait_ge(mt_ready, a + 1)
                    mm(self_at("shift")[0:64, 0:SEG], mt[:].rearrange("n s t h -> n (s t h)"), stack_b[:]).then_inc(self_fill("shift"), 1)
                    pe.wait_ge(shift_ready, a + 1)
                    for t in range(4):
                        wait(pe, self_free(f"score{t}", a))
                        for n in range(4):
                            pair, s = 2 * t + n // 2, n % 2
                            p = self_at(f"score{t}")[0:KEYS, 128 * n:128 * (n + 1)]
                            mm(p, kall[:, pair, s, :], qpad[:, pair, s, :, :].rearrange("p h i -> p (h i)"), stop=False)
                            for h in range(2):
                                last = mm(p[:, SEG * h:SEG * (h + 1)], select_b[:, (2 * pair + h) * NSEG + s, :], shift_b[:], start=False)
                        last.then_inc(self_fill(f"score{t}"), 1)
                if c is not None:
                    wait(pe, cross_free("wo", c))
                    pe.wait_ge(c0T_ready, c + 1)
                    mm(cross_at("wo")[:, 0:D], c0T[:], wo[:]).then_inc(cross_fill("wo"), 1)
                if a is not None:
                    pe.wait_ge(v_ready, a * 2 + 2)
                    pe.wait_ge(memv_in, a * 32 + 32)
                    for t in range(4):
                        wait(pe, self_free(f"pv{t}", a))
                        if t == 3:
                            pe.wait_ge(probs_ready, a * 4 + (t + 1))
                        for n in range(4):
                            pair, h = 2 * t + n // 2, n % 2
                            for s in range(NSEG):
                                w = VW * (4 * t + n)
                                last = mm(self_at(f"pv{t}")[SEG * s:SEG * (s + 1), PVN * n:PVN * (n + 1)],
                                          probs[:, pair, s, h, :], vall[s][:, w:w + PVN])
                        last.then_inc(self_fill(f"pv{t}"), 1)
                    for t in range(2):
                        pe.wait_ge(o_ready, a * 4 + (2 * t + 2))
                        for n in range(4):
                            pair = 4 * t + n
                            last = nc.tensor.transpose(self_at(f"oT{t}")[:, 128 * n:128 * (n + 1)],
                                                       o[:, 2 * pair:2 * pair + 2, :].rearrange("n h d -> n (h d)"), ident[:])
                        last.then_inc(self_fill(f"oT{t}"), 1)
                    wait(pe, self_free("out", a))
                    for n in range(PAIRS):
                        if n % 4 == 0:
                            pe.wait_ge(oT_ready, a * 2 + (n // 4 + 1))
                        last = mm(self_at("out")[:, 0:D], oT[:, n, :], wout[:, n, :], start=n == 0, stop=n == PAIRS - 1)
                    last.then_inc(self_fill("out"), 1)

            pipeline(pe, body)
    return nc


def constants():
    f = np.float32
    inv = (f(1.0) / f(10000.0) ** (np.arange(0, DH, 2, dtype=f) / f(DH))).astype(f)
    ang = (np.arange(S, dtype=f)[:, None] * inv[None, :]).astype(f).astype(np.float64)
    cos, sin = np.cos(ang), np.sin(ang)
    rope = np.stack([np.repeat(cos, 2, 1), np.stack([-sin, sin], -1).reshape(S, DH)], 1).astype(f)
    headmask = (np.arange(D)[:, None] // HD0 == np.arange(H)[None, :]).astype(f)
    i = np.arange(SEG)
    causal = np.tile(np.where(i[None, :] > i[:, None], NEG, 0.0), (NSEG, 1)).astype(f)
    stack = np.tile(np.eye(SEG), (NSEG, 1)).astype(f)
    shift = np.concatenate([np.zeros((64, SEG)), np.where(i[:, None] > i[None, :], NEG, 0.0)]).astype(f)
    select = np.zeros((128, H, NSEG, KEYS), f)
    for s in range(NSEG):
        for part in range(2):
            for h in range(H):
                select[s * 32 + part * 16 + h, h, s, :] = 1.0
    for j in range(SEG):
        select[64 + j, :, :, j] = 1.0
    return {"c_ident": np.eye(128, dtype=f), "c_rope": rope, "c_headmask": headmask, "c_causal": causal,
            "c_shift": shift, "c_select": select.reshape(128, -1), "c_stack": stack}


INPUTS = ["x", "ctx_1024", "mask_Bx1xSxS2_fk0"] + [f"L0_xattn_{n}" for n in ("Wq", "bq", "Wk", "bk", "Wv", "bv", "Wo", "bo", "gamma", "beta")] + [
    f"L1_xattn_{n}" for n in ("attn_norm_w", "to_qkv_w", "to_out_w", "persist_mem", "mem_pool_norm_w", "to_mem_tokens_w",
                              "ff_norm_w", "ff_w1", "ff_b1", "ff_w2", "ff_b2")]


def kernel(**inputs):
    import concourse.bacc as bacc
    from concourse.bass_utils import run_bass_kernel_spmd

    nc = bacc.Bacc("TRN2", target_bir_lowering=False, num_devices=1)
    arrays, args = {}, []
    for name, value in [(n, inputs[n]) for n in INPUTS] + list(constants().items()):
        value = np.ascontiguousarray(value)
        arrays[f"in_{name}"] = value
        args.append(nc.dram_tensor(f"in_{name}", value.shape, mybir.dt.from_np(value.dtype), kind="ExternalInput").ap())
    out = nc.dram_tensor("out", (B, S, D), F32, kind="ExternalOutput").ap()
    build(nc, *args, out)
    return run_bass_kernel_spmd(nc, [arrays], core_ids=[0]).results[0]["out"]
```

```python
from contextlib import ExitStack
from functools import partial

import numpy as np

import concourse.bass as bass
from concourse import mybir

ALU = mybir.AluOpType
ACT = mybir.ActivationFunctionType
F32 = mybir.dt.float32
BF16 = mybir.dt.bfloat16
AX_X = mybir.AxisListType.X

B, S, D = 64, 128, 128
S2 = 77
H = 16
HD0 = D // H
DH = 64
INNER = H * DH
PAIRS = H // 2
SEG = 64
NSEG = S // SEG
NPM, NM = 16, 16
PRE = 1 + NPM
KEYS = SEG + PRE
VW = DH + 1
PVN = 96
DFF = 341
FCH = 3
FROWS = [128, 128, DFF - 256]
LN_EPS, RMS_EPS = 1e-5, 1.1920929e-07
CLAMP = 50.0
BANK = 512
NEG = -1e30
QK = ("q0", "k0", "q1", "k1")


def banks(ctx, nc, psum, stage, first_bank, n_banks, tasks):
    names = [t[0] for t in tasks]
    fills = [ctx.enter_context(nc.semaphore(f"{stage}_bank{first_bank + n}_filled")) for n in range(n_banks)]

    def at(task):
        return psum[:, first_bank + names.index(task) % n_banks, :]

    def fill(task):
        return fills[names.index(task) % n_banks]

    def is_filled(task, seq):
        n = names.index(task)
        uses = len(range(n % n_banks, len(names), n_banks))
        return fill(task), seq * uses + (n // n_banks + 1)

    def is_free(task, seq):
        n = names.index(task)
        if n >= n_banks:
            _, read, k, per_seq = tasks[n - n_banks]
            return read, seq * per_seq + k
        _, read, k, per_seq = tasks[max(range(n, len(names), n_banks))]
        return read, 0 if first(seq) else seq * per_seq + (k - per_seq)

    return at, fill, is_filled, is_free


def steps(semaphore, *names):
    return semaphore, lambda name, seq: seq * len(names) + (names.index(name) + 1)


def wait(eng, signal_count):
    signal, count = signal_count
    if not (isinstance(count, int) and count <= 0):
        eng.wait_ge(signal, count)


def passed(eng, signal):
    eng.sem_inc(signal, 1)


def first(seq):
    return isinstance(seq, int) and seq == 0


def build(nc, x, ctx_in, mask, Wq, bq, Wk, bk, Wv, bv, Wo, bo, gamma, beta, attn_norm_w, to_qkv_w,
          to_out_w, persist_mem, mem_pool_norm_w, to_mem_tokens_w, ff_norm_w, ff_w1, ff_b1, ff_w2, ff_b2,
          c_ident, c_rope, c_headmask, c_causal, c_shift, c_select, c_stack, out):
    with ExitStack() as ctx:
        def sb(name, shape, dt=F32):
            return ctx.enter_context(nc.sbuf_tensor(name, shape, dt))

        def sem(name):
            return ctx.enter_context(nc.semaphore(name))

        psum = ctx.enter_context(nc.psum_tensor("psum", [128, 8, BANK], F32))
        memv_dram = nc.dram_tensor("memv_dram", (B, INNER), F32, kind="Internal").ap()

        wq, wk, wv, wo = (sb(n, [D, D]) for n in ("wq", "wk", "wv", "wo"))
        wqkv = sb("wqkv", [D, 3 * INNER])
        wout = sb("wout", [128, PAIRS, D])
        wmem = sb("wmem", [D, D])
        w1 = sb("w1", [D, 2 * DFF])
        w2 = sb("w2", [128, FCH, D])
        cols = sb("cols", [128, 12])
        BQ, BK, NW, PW, FW = range(5)
        ff_bias = sb("ff_bias", [128, 2, FCH])
        half_bg = sb("half_bg", [128, FCH])
        bv_rep, bo_rep, ga_rep, be_rep, b2_rep = (sb(n, [128, D]) for n in ("bv_rep", "bo_rep", "ga_rep", "be_rep", "b2_rep"))
        ident = sb("ident", [128, 128])
        ident_b = sb("ident_b", [128, 128], BF16)
        rope = sb("rope", [128, 2, DH])
        headmask = sb("headmask", [128, H])
        causal_b = sb("causal_b", [128, SEG], BF16)
        select_b = sb("select_b", [128, H * NSEG, KEYS], BF16)
        stack_b = sb("stack_b", [128, SEG], BF16)
        shift_b = sb("shift_b", [128, SEG], BF16)

        x_sb = sb("x_sb", [S, D])
        ctx_sb = sb("ctx_sb", [S2, D])
        mask_sb = sb("mask_sb", [S, S2])
        xT = sb("xT", [D, S])
        ctxT = sb("ctxT", [D, S2])
        wT = sb("wT", [S2, S])
        xb = sb("xb", [S, D])
        q0T = sb("q0T", [D, S])
        kpad = sb("kpad", [D, H, S2])
        VB = 4 * HD0 + 40
        v0 = sb("v0", [S2, 4, 4, VB])
        z0 = sb("z0", [S2, H, S])
        rden0 = sb("rden0", [128, 2 * S])
        c0T = sb("c0T", [D, S])
        r0 = sb("r0", [S, D])
        t0g = sb("t0g", [S, D])
        y = sb("y", [S, D])
        ysq = sb("ysq", [S, D])
        xn = sb("xn", [S, D])
        st0 = sb("st0", [S, 16])
        bn0 = sb("bn0", [S, 6])

        y_keep = sb("y_keep", [S, D])
        xnT = sb("xnT", [D, S])
        ra = sb("ra", [S, 2 * INNER])
        rb = sb("rb", [S, 2 * INNER])
        qpad = sb("qpad", [128, PAIRS, NSEG, 2, SEG])
        kall = sb("kall", [128, PAIRS, NSEG, KEYS])
        memk = sb("memk", [128, B, PAIRS])
        vall = [sb(f"vall{s}", [KEYS, H * VW + PVN - VW]) for s in range(NSEG)]
        mx = sb("mx", [S, H])
        mt = sb("mt", [S, NSEG, 2, H], BF16)
        probs = sb("probs", [KEYS, PAIRS, NSEG, 2, SEG])
        rden1 = sb("rden1", [S, H])
        o = sb("o", [S, H, DH])
        oT = sb("oT", [128, PAIRS, S])
        x1 = sb("x1", [S, D])
        x1sq = sb("x1sq", [S, D])
        hn = sb("hn", [S, D])
        st1 = sb("st1", [S, 8])

        hnT = sb("hnT", [D, S])
        half_gate = sb("half_gate", [128, FCH, S])
        tanh_gate = sb("tanh_gate", [128, FCH, S])
        ug = sb("ug", [128, FCH, S])
        sT = sb("sT", [128, FCH, S])
        x1b = sb("x1b", [S, D])
        out_sb = sb("out_sb", [S, D])

        ctx_all = sb("ctx_all", [S2, B, D])
        stage = sb("stage", [128, H * NSEG * KEYS])
        stage2 = sb("stage2", [128, 3 * SEG])
        ones = sb("ones", [S2, 1])
        nhalf = sb("nhalf", [128, 1])
        pm_sb = sb("pm_sb", [NPM, INNER])
        pool_T = sb("pool_T", [D, B])
        pool_n = sb("pool_n", [B, 3, D])
        pool_st = sb("pool_st", [B, 4])
        pool_nT = sb("pool_nT", [D, B])
        memT = sb("memT", [D, B])
        memv = sb("memv", [B, INNER])

        w_in = sem("w_in")
        ctx_all_in = sem("ctx_all_in")
        pm_v_in = sem("pm_v_in")
        zeros_step = sem("zeros_step")
        zeros_set = sem("zeros_set")
        consts_cast = sem("consts_cast")
        setup_pe, setup_act, setup_dve, setup_pool = sem("setup_pe"), sem("setup_act"), sem("setup_dve"), sem("setup_pool")
        memv_stored = sem("memv_stored")
        dve_passed, pool_passed, sp_passed = sem("dve_passed"), sem("pool_passed"), sem("sp_passed")
        x_in, ctx_loaded, mask_in = sem("x_in"), sem("ctx_loaded"), sem("mask_in")
        inT_ready = sem("inT_ready")
        xb_ready = sem("xb_ready")
        qkv0_ready = sem("qkv0_ready")
        z_ready = sem("z_ready")
        clip_ready = sem("clip_ready")
        exp0_ready = sem("exp0_ready")
        c0T_ready = sem("c0T_ready")
        var0_ready, rstd0_ready = sem("var0_ready"), sem("rstd0_ready")
        ms0_ready, rms0_ready = sem("ms0_ready"), sem("rms0_ready")
        ms1_ready, rms1_ready = sem("ms1_ready"), sem("rms1_ready")
        centred_ready = sem("centred_ready")
        r_ready = sem("r_ready")
        xn_ready = sem("xn_ready")
        cross_step = sem("cross_step")
        ykeep_ready = sem("ykeep_ready")
        xnT_ready = sem("xnT_ready")
        rope_ready = sem("rope_ready")
        rot_ready = sem("rot_ready")
        qk_ready = sem("qk_ready")
        memk_ready = sem("memk_ready")
        memv_in = sem("memv_in")
        v_ready = sem("v_ready")
        max_ready = sem("max_ready")
        mt_ready = sem("mt_ready")
        shift_ready = sem("shift_ready")
        probs_ready = sem("probs_ready")
        o_ready = sem("o_ready")
        oT_ready = sem("oT_ready")
        x1_ready = sem("x1_ready")
        hn_ready = sem("hn_ready")
        self_step = sem("self_step")
        hnT_ready = sem("hnT_ready")
        x1b_ready = sem("x1b_ready")
        gate_ready = sem("gate_ready")
        sT_ready = sem("sT_ready")
        silu_ready = sem("silu_ready")
        out_ready = sem("out_ready")
        out_stored = sem("out_stored")

        cross_at, cross_fill, cross_filled, cross_free = banks(ctx, nc, psum, "cross", 0, 2, [
            ("inT", inT_ready, 1, 1), ("qkv", qkv0_ready, 1, 1), *[(f"score{t}", z_ready, t + 1, 4) for t in range(4)],
            ("pv", c0T_ready, 1, 1), ("wo", r_ready, 1, 1)])
        self_at, self_fill, self_filled, self_free = banks(ctx, nc, psum, "self", 2, 4, [
            ("xnT", xnT_ready, 1, 1), ("q0", rope_ready, 1, 4), ("k0", rope_ready, 2, 4), ("v0", v_ready, 1, 2),
            ("q1", rope_ready, 3, 4), ("k1", rope_ready, 4, 4), ("v1", v_ready, 2, 2),
            *[(f"{name}T", qk_ready, t + 1, 4) for t, name in enumerate(QK)], *[(f"max{t}", max_ready, t + 1, 4) for t in range(4)],
            *[(f"score{t}", probs_ready, t + 1, 4) for t in range(3)], ("shift", shift_ready, 1, 1), ("score3", probs_ready, 4, 4),
            *[(f"pv{t}", o_ready, t + 1, 4) for t in range(4)], *[(f"oT{t}", oT_ready, t + 1, 2) for t in range(2)],
            ("out", x1_ready, 1, 1)])
        ff_at, ff_fill, ff_filled, ff_free = banks(ctx, nc, psum, "ff", 6, 2, [
            ("hnT", hnT_ready, 1, 1), ("gate", gate_ready, 1, 1), ("lin", sT_ready, 1, 1), ("down", out_ready, 1, 1)])
        cross_steps = steps(cross_step, "rden", "bn", "mean", "y")
        self_steps = steps(self_step, "hi", *[f"rden{t}" for t in range(4)])

        weight_loads = [
            (wq[:], Wq), (wk[:], Wk), (wv[:], Wv), (wo[:], Wo), (wqkv[:], to_qkv_w),
            (wout[:], to_out_w.rearrange("(c p) n -> p c n", p=128)), (wmem[:], to_mem_tokens_w), (w1[:], ff_w1),
            (w2[:, 0:2, :], ff_w2[0:256, :].rearrange("(c p) n -> p c n", p=128)), (w2[0:FROWS[2], 2, :], ff_w2[256:DFF, :]),
            (ident[:], c_ident), (rope[:], c_rope), (headmask[:], c_headmask),
            (stage2[:, 0:SEG], c_causal), (stage2[:, SEG:2 * SEG], c_stack), (stage2[:, 2 * SEG:3 * SEG], c_shift),
            (stage[:], c_select), (pm_sb[:].rearrange("n (h d) -> n h d", h=H), persist_mem.rearrange("h n d -> n h d")),
        ]
        weight_loads += [(cols[:, n:n + 1], v.rearrange("(p a) -> p a", a=1))
                         for n, v in ((BQ, bq), (BK, bk), (NW, attn_norm_w), (PW, mem_pool_norm_w), (FW, ff_norm_w))]
        for part in range(2):
            for c in range(FCH):
                lo = part * DFF + 128 * c
                weight_loads.append((ff_bias[0:FROWS[c], part, c:c + 1],
                                     ff_b1[lo:lo + FROWS[c]].rearrange("(p a) -> p a", a=1)))
        weight_loads += [(t[:], v.rearrange("(a n) -> a n", a=1).broadcast_to([128, D]))
                         for t, v in ((bv_rep, bv), (bo_rep, bo), (ga_rep, gamma), (be_rep, beta), (b2_rep, ff_b2))]
        WEIGHTS_IN = 16 * len(weight_loads)

        def columns(name):
            lo = INNER * (name[0] == "k") + BANK * int(name[1])
            return slice(lo, lo + BANK)

        block = ctx.enter_context(nc.Block())

        def pipeline(eng, body):
            body(0, None, None)
            body(1, 0, None)
            body(2, 1, 0)
            with eng.Fori(1, B - 2) as i:
                body(i + 2, i + 1, i)
            body(None, B - 1, B - 2)
            body(None, None, B - 1)

        @block.sync
        def _(sp):
            sp.dma_start(ctx_all[:], ctx_in.rearrange("b s d -> s b d")).then_inc(ctx_all_in, 16)
            for dst, src in weight_loads:
                sp.dma_start(dst, src).then_inc(w_in, 16)
            sp.wait_ge(zeros_set, 2)
            for s in range(NSEG):
                sp.dma_start(vall[s][SEG + 1:KEYS, 0:H * VW].rearrange("n (h w) -> n h w", h=H)[:, :, 0:DH],
                             persist_mem.rearrange("h n d -> n h d")).then_inc(pm_v_in, 16)
            sp.wait_ge(setup_act, 7)
            sp.dma_start(memv_dram, memv[:]).then_inc(memv_stored, 16)
            sp.wait_ge(memv_stored, 16)

            def body(c, a, f):
                if c is not None:
                    if not first(c):
                        wait(sp, cross_filled("inT", c - 1))
                        passed(sp, sp_passed)
                    wait(sp, (xb_ready, c))
                    passed(sp, sp_passed)
                    sp.dma_start(x_sb[:], x[bass.ds(c, 1), :, :].rearrange("b s d -> (b s) d")).then_inc(x_in, 16)
                    sp.dma_start(ctx_sb[:], ctx_in[bass.ds(c, 1), :, :].rearrange("b s d -> (b s) d")).then_inc(ctx_loaded, 16)
                    sp.dma_start(mask_sb[:], mask[bass.ds(c, 1), :, :, :].rearrange("b u s k -> (b u s) k")).then_inc(mask_in, 16)
                if a is not None:
                    if not first(a):
                        wait(sp, self_filled("pv3", a - 1))
                        passed(sp, sp_passed)
                    for s in range(NSEG):
                        sp.dma_start(vall[s][SEG:SEG + 1, 0:H * VW].rearrange("n (h w) -> n h w", h=H)[:, :, 0:DH],
                                     memv_dram[bass.ds(a, 1), :].rearrange("b (h d) -> b h d", h=H)).then_inc(memv_in, 16)
                if f is not None:
                    sp.wait_ge(out_ready, f + 1)
                    passed(sp, sp_passed)
                    sp.dma_start(out[bass.ds(f, 1), :, :].rearrange("b s d -> (b s) d"), out_sb[:]).then_inc(out_stored, 16)

            pipeline(sp, body)
            sp.wait_ge(out_stored, 16 * B)

        @block.gpsimd
        def _(pool):
            for t in (*vall, qpad, kpad, v0, mt, half_gate, tanh_gate):
                nc.gpsimd.memset(t[:], 0.0).then_inc(zeros_step, 1)
            pool.wait_ge(zeros_step, 8)
            nc.gpsimd.memset(ones[:], 1.0)
            nc.gpsimd.memset(nhalf[:], -0.5)
            nc.gpsimd.memset(v0[:, :, :, 4 * HD0:5 * HD0], 1.0)
            for s in range(NSEG):
                nc.gpsimd.memset(vall[s][:, 0:H * VW].rearrange("n (h w) -> n h w", h=H)[:, :, DH:VW], 1.0).then_inc(zeros_step, 1)
            pool.wait_ge(zeros_step, 10)
            for s in range(NSEG):
                mem_col = vall[s][SEG:SEG + 1, 0:H * VW].rearrange("n (h w) -> n h w", h=H)[:, :, DH:VW]
                nc.gpsimd.memset(mem_col, float(NM)).then_inc(zeros_set, 1)
            pool.wait_ge(w_in, WEIGHTS_IN)
            pool.wait_ge(setup_dve, 3)
            nc.gpsimd.tensor_tensor(pool_st[:, 2:3], pool_st[:, 1:2], nhalf[0:B, :], ALU.pow).then_inc(setup_pool, 1)
            pool.wait_ge(setup_act, 7)

            def body(c, a, f):
                if f is not None:
                    pool.wait_ge(x1_ready, f + 1)
                    wait(pool, (out_ready, f))
                    nc.gpsimd.tensor_tensor(x1b[:], x1[:], b2_rep[:], ALU.add).then_inc(x1b_ready, 1)
                if a is not None:
                    pool.wait_ge(xn_ready, a + 1)
                    wait(pool, (x1_ready, a))
                    passed(pool, pool_passed)
                    nc.gpsimd.tensor_scalar(y_keep[:], y[:], 1.0, 0.0, ALU.mult, ALU.add).then_inc(ykeep_ready, 1)
                if c is not None:
                    pool.wait_ge(x_in, (c + 1) * 16)
                    wait(pool, (xn_ready, c))
                    nc.gpsimd.tensor_tensor(xb[:], x_sb[:], bo_rep[:], ALU.add).then_inc(xb_ready, 1)
                if a is not None:
                    if not first(a):
                        wait(pool, self_filled("score3", a - 1))
                    mk = memk[:, bass.ds(a, 1), :].rearrange("p b c -> p c b").unsqueeze(2).broadcast_to([128, PAIRS, NSEG, 1])
                    nc.gpsimd.tensor_copy(kall[:, :, :, SEG:SEG + 1], mk).then_inc(memk_ready, 1)
                    for t, name in enumerate(QK):
                        pool.wait_ge(rope_ready, a * 4 + (t + 1))
                        sl = columns(name)
                        nc.gpsimd.tensor_tensor(ra[:, sl], ra[:, sl], rb[:, sl], ALU.add).then_inc(rot_ready, 1)
                if c is not None:
                    pool.wait_ge(var0_ready, c + 1)
                    nc.gpsimd.tensor_tensor(st0[:, 3:4], st0[:, 2:3], nhalf[:], ALU.pow).then_inc(rstd0_ready, 1)
                    pool.wait_ge(ms0_ready, c + 1)
                    nc.gpsimd.tensor_tensor(st0[:, 6:7], st0[:, 4:5], nhalf[:], ALU.pow).then_inc(rms0_ready, 1)
                if a is not None:
                    pool.wait_ge(ms1_ready, a + 1)
                    nc.gpsimd.tensor_tensor(st1[:, 2:3], st1[:, 0:1], nhalf[:], ALU.pow).then_inc(rms1_ready, 1)

            pipeline(pool, body)

        @block.scalar
        def _(act):
            copy = lambda out, in_, **k: nc.scalar.activation(out, in_, ACT.Copy, **k)
            bank = lambda n: psum[:, n, :]
            act.wait_ge(w_in, WEIGHTS_IN)
            for n in range(FCH):
                nc.scalar.mul(half_bg[0:FROWS[n], n:n + 1], ff_bias[0:FROWS[n], 1, n:n + 1], 0.5)
            act.wait_ge(setup_pe, 1)
            copy(pool_T[:], bank(0)[:, 0:B], scale=1.0 / S2).then_inc(setup_act, 1)
            act.wait_ge(setup_pe, 3)
            copy(pool_nT[:], bank(2)[:, 0:B], scale=cols[:, PW:PW + 1]).then_inc(setup_act, 1)
            act.wait_ge(setup_pe, 4)
            copy(memT[:], bank(3)[:, 0:B]).then_inc(setup_act, 1)
            act.wait_ge(setup_pe, 5)
            copy(memk[:].rearrange("p b c -> p c b"), bank(4).rearrange("p (c b) -> p c b", c=PAIRS)).then_inc(setup_act, 1)
            for t in range(2):
                copy(memv[:, BANK * t:BANK * (t + 1)], bank(5 + t)[0:B, :], scale=float(NM)).then_inc(setup_act, 1)
            pk = bank(7)[:, 0:PAIRS * NPM].rearrange("p (c n) -> p c n", c=PAIRS)
            for s in range(NSEG):
                last = copy(kall[:, :, s, SEG + 1:KEYS], pk)
            last.then_inc(setup_act, 1)
            act.wait_ge(zeros_set, 2)

            def body(c, a, f):
                def values(t):
                    wait(act, self_filled(f"v{t}", a))
                    for s in range(NSEG):
                        dst = vall[s][0:SEG, VW * 8 * t:VW * 8 * (t + 1)].rearrange("n (h w) -> n h w", h=8)[:, :, 0:DH]
                        last = copy(dst, self_at(f"v{t}")[SEG * s:SEG * (s + 1), :].rearrange("n (h d) -> n h d", h=8))
                    last.then_inc(v_ready, 1)

                def turned(name):
                    wait(act, self_filled(f"{name}T", a))
                    p, pairs = self_at(f"{name}T"), slice(4 * int(name[1]), 4 * int(name[1]) + 4)
                    if name[0] == "k":
                        last = copy(kall[:, pairs, :, 0:SEG], p.rearrange("p (c s j) -> p c s j", c=4, s=NSEG))
                    else:
                        for h in range(2):
                            rows = slice(DH * h, DH * (h + 1))
                            last = copy(qpad[rows, pairs, :, h, :], p[rows, :].rearrange("p (c s i) -> p c s i", c=4, s=NSEG))
                    last.then_inc(qk_ready, 1)

                def exp_cross(t):
                    act.wait_ge(clip_ready, c * 4 + (t + 1))
                    zt = z0[:, 4 * t:4 * t + 4, :]
                    nc.scalar.activation(zt, zt, ACT.Exp, scale=float(HD0) ** -0.5).then_inc(exp0_ready, 1)

                if a is not None:
                    wait(act, self_filled("xnT", a))
                    copy(xnT[:], self_at("xnT")[:, 0:S], scale=cols[:, NW:NW + 1]).then_inc(xnT_ready, 1)
                if c is not None:
                    wait(act, cross_filled("inT", c))
                    wait(act, (z_ready, c * 4))
                    p = cross_at("inT")
                    copy(xT[:], p[:, 0:S])
                    copy(ctxT[:], p[:, S:S + S2])
                    copy(wT[:], p[0:S2, 256:256 + S], scale=0.5, bias=0.5).then_inc(inT_ready, 1)
                if a is not None:
                    values(0)
                if f is not None:
                    wait(act, ff_filled("hnT", f))
                    copy(hnT[:], ff_at("hnT")[:, 0:S], scale=cols[:, FW:FW + 1]).then_inc(hnT_ready, 1)
                if a is not None:
                    values(1)
                if f is not None:
                    wait(act, ff_filled("gate", f))
                    for n in range(FCH):
                        m = FROWS[n]
                        for dst, function in ((tanh_gate, ACT.Tanh), (half_gate, ACT.Identity)):
                            last = nc.scalar.activation(dst[0:m, n, :], ff_at("gate")[0:m, S * n:S * (n + 1)], function,
                                                        scale=0.5, bias=half_bg[0:m, n:n + 1])
                    last.then_inc(gate_ready, 1)
                if c is not None:
                    exp_cross(0)
                    exp_cross(1)
                if a is not None:
                    turned("q0")
                if c is not None:
                    exp_cross(2)
                if a is not None:
                    turned("k0")
                if c is not None:
                    exp_cross(3)
                if a is not None:
                    turned("q1")
                    turned("k1")
                    for t in range(4):
                        wait(act, self_filled(f"score{t}", a))
                        nc.scalar.activation(probs[:, 2 * t:2 * t + 2, :, :, :].rearrange("k c s h i -> k (c s h i)"),
                                             self_at(f"score{t}")[0:KEYS, :], ACT.Exp, scale=float(DH) ** -0.5).then_inc(probs_ready, 1)
                    for t in range(2):
                        wait(act, self_filled(f"oT{t}", a))
                        copy(oT[:, 4 * t:4 * t + 4, :].rearrange("p c s -> p (c s)"), self_at(f"oT{t}")).then_inc(oT_ready, 1)

            pipeline(act, body)

        @block.vector
        def _(dve):
            V = nc.vector

            def then(ins, steps_of, name, seq):
                semaphore, done = steps_of
                ins.then_inc(semaphore, 1)
                wait(dve, (semaphore, done(name, seq)))

            dve.wait_ge(w_in, WEIGHTS_IN)
            V.tensor_copy(ident_b[:], ident[:])
            V.tensor_copy(causal_b[:], stage2[:, 0:SEG])
            V.tensor_copy(stack_b[:], stage2[:, SEG:2 * SEG])
            V.tensor_copy(shift_b[:], stage2[:, 2 * SEG:3 * SEG])
            V.tensor_copy(select_b[:].rearrange("p n k -> p (n k)"), stage[:]).then_inc(consts_cast, 1)
            dve.wait_ge(setup_pe, 2)
            V.tensor_copy(pool_n[:, 0, :], psum[0:B, 1, 0:D]).then_inc(setup_dve, 1)
            dve.wait_ge(setup_dve, 1)
            V.tensor_tensor_reduce(out=pool_n[:, 1, :], in0=pool_n[:, 0, :], in1=pool_n[:, 0, :], scale=1.0, scalar=0.0,
                                   op0=ALU.mult, op1=ALU.add, accum_out=pool_st[:, 0:1]).then_inc(setup_dve, 1)
            dve.wait_ge(setup_dve, 2)
            V.tensor_scalar(pool_st[:, 1:2], pool_st[:, 0:1], 1.0 / D, RMS_EPS, ALU.mult, ALU.add).then_inc(setup_dve, 1)
            dve.wait_ge(setup_pool, 1)
            V.tensor_scalar(pool_n[:, 2, :], pool_n[:, 0, :], pool_st[:, 2:3], None, ALU.mult).then_inc(setup_dve, 1)
            dve.wait_ge(zeros_set, 2)

            def body(c, a, f):
                def rotary(name):
                    wait(dve, self_filled(name, a))
                    sl = columns(name)
                    p = self_at(name).rearrange("n (h d) -> n h d", h=8)
                    V.tensor_tensor(ra[:, sl].rearrange("n (h d) -> n h d", h=8), p,
                                    rope[:, 0, :].unsqueeze(1).broadcast_to([S, 8, DH]), ALU.mult)
                    p = self_at(name).rearrange("n (h e t) -> n h e t", h=8, t=2)[:, :, :, ::-1]
                    V.tensor_tensor(rb[:, sl].rearrange("n (h e t) -> n h e t", h=8, t=2), p,
                                    rope[:, 1, :].rearrange("n (e t) -> n e t", t=2).unsqueeze(1).broadcast_to([S, 8, DH // 2, 2]),
                                    ALU.mult).then_inc(rope_ready, 1)

                def masked(t):
                    wait(dve, cross_filled(f"score{t}", c))
                    V.tensor_tensor(z0[:, 4 * t:4 * t + 4, :], cross_at(f"score{t}")[0:S2, :].rearrange("k (h q) -> k h q", h=4),
                                    wT[:].unsqueeze(1).broadcast_to([S2, 4, S]), ALU.mult).then_inc(z_ready, 1)

                def clamped(t):
                    lim = CLAMP * float(HD0) ** 0.5
                    zt = z0[:, 4 * t:4 * t + 4, :]
                    dve.wait_ge(z_ready, c * 4 + (t + 1))
                    passed(dve, dve_passed)
                    V.tensor_scalar(zt, zt, lim, -lim, ALU.min, ALU.max).then_inc(clip_ready, 1)

                def normalised(t):
                    wait(dve, self_filled(f"pv{t}", a))
                    p = self_at(f"pv{t}")[:, 0:4 * PVN].rearrange("n (h w) -> n h w", h=4)
                    then(V.reciprocal(rden1[:, 4 * t:4 * t + 4].unsqueeze(2), p[:, :, DH:VW]), self_steps, f"rden{t}", a)
                    V.tensor_tensor(o[:, 4 * t:4 * t + 4, :], p[:, :, 0:DH],
                                    rden1[:, 4 * t:4 * t + 4].unsqueeze(2).broadcast_to([S, 4, DH]), ALU.mult).then_inc(o_ready, 1)

                if a is not None:
                    rotary("q0")
                    rotary("k0")
                if c is not None:
                    wait(dve, cross_filled("qkv", c))
                    p = cross_at("qkv")
                    V.tensor_scalar(q0T[:], p[:, 0:S], cols[:, BQ:BQ + 1], None, ALU.add)
                    V.scalar_tensor_tensor(out=kpad[:], in0=p[:, S:S + S2].unsqueeze(1).broadcast_to([D, H, S2]),
                                           scalar=cols[:, BK:BK + 1], in1=headmask[:].unsqueeze(2).broadcast_to([D, H, S2]),
                                           op0=ALU.add, op1=ALU.mult)
                    V.tensor_tensor(v0[:, :, :, 0:HD0], p[0:S2, 256:384].rearrange("k (g r d) -> k g r d", g=4, r=4),
                                    bv_rep[0:S2, :].rearrange("k (g r d) -> k g r d", g=4, r=4), ALU.add).then_inc(qkv0_ready, 1)
                if a is not None:
                    rotary("q1")
                    rotary("k1")
                if c is not None:
                    dve.wait_ge(inT_ready, c + 1)
                    masked(0)
                    masked(1)
                    clamped(0)
                if f is not None:
                    dve.wait_ge(gate_ready, f + 1)
                    V.scalar_tensor_tensor(out=ug[:], in0=tanh_gate[:], scalar=1.0, in1=half_gate[:],
                                           op0=ALU.add, op1=ALU.mult).then_inc(silu_ready, 1)
                if c is not None:
                    clamped(1)
                    masked(2)
                if f is not None:
                    wait(dve, ff_filled("lin", f))
                    dve.wait_ge(silu_ready, f + 1)
                    for n in range(FCH):
                        m = FROWS[n]
                        last = V.scalar_tensor_tensor(out=sT[0:m, n, :], in0=ff_at("lin")[0:m, S * n:S * (n + 1)],
                                                      scalar=ff_bias[0:m, 0, n:n + 1], in1=ug[0:m, n, :], op0=ALU.add, op1=ALU.mult)
                    last.then_inc(sT_ready, 1)
                if c is not None:
                    masked(3)
                    clamped(2)
                    clamped(3)
                if f is not None:
                    wait(dve, ff_filled("down", f))
                    dve.wait_ge(x1b_ready, f + 1)
                    wait(dve, (out_stored, f * 16))
                    V.tensor_tensor(out_sb[:], ff_at("down")[:, 0:D], x1b[:], ALU.add).then_inc(out_ready, 1)
                if c is not None:
                    wait(dve, cross_filled("pv", c))
                    p = cross_at("pv")
                    then(V.reciprocal(rden0[:], p[:, 0:2 * S]), cross_steps, "rden", c)
                    for g in range(4):
                        half, q = 64 * (g % 2), slice(S * (g // 2), S * (g // 2 + 1))
                        last = V.tensor_tensor(c0T[32 * g:32 * g + 32, :], p[half:half + 32, q], rden0[half + 32:half + 64, q], ALU.mult)
                    last.then_inc(c0T_ready, 1)
                if a is not None:
                    for t in range(4):
                        wait(dve, self_filled(f"max{t}", a))
                        V.reduce_max(mx[:, 4 * t:4 * t + 4], self_at(f"max{t}")[:, 0:4 * KEYS].rearrange("n (h k) -> n h k", h=4),
                                     AX_X).then_inc(max_ready, 1)
                    dve.wait_ge(max_ready, a * 4 + 4)
                    for s in range(NSEG):
                        rows = slice(SEG * s, SEG * (s + 1))
                        last = V.tensor_scalar(mt[rows, s, 0, :], mx[rows, :], -1.0, None, ALU.mult)
                    then(last, self_steps, "hi", a)
                    for s in range(NSEG):
                        rows = slice(SEG * s, SEG * (s + 1))
                        last = V.scalar_tensor_tensor(out=mt[rows, s, 1, :], in0=mx[rows, :], scalar=-1.0, in1=mt[rows, s, 0, :],
                                                      op0=ALU.mult, op1=ALU.subtract)
                    last.then_inc(mt_ready, 1)
                    wait(dve, self_filled("shift", a))
                    V.tensor_copy(shift_b[0:64, :], self_at("shift")[0:64, 0:SEG]).then_inc(shift_ready, 1)
                if c is not None:
                    wait(dve, cross_filled("wo", c))
                    dve.wait_ge(xb_ready, c + 1)
                    V.tensor_tensor(r0[:], cross_at("wo")[:, 0:D], xb[:], ALU.add).then_inc(r_ready, 1)
                    dve.wait_ge(r_ready, c + 1)
                    then(V.bn_stats(bn0[:], r0[:]), cross_steps, "bn", c)
                    passed(dve, dve_passed)
                    then(V.bn_aggr(st0[:, 0:2], bn0[:]), cross_steps, "mean", c)
                    V.tensor_scalar(st0[:, 2:3], st0[:, 1:2], LN_EPS, None, ALU.add).then_inc(var0_ready, 1)
                    V.scalar_tensor_tensor(out=t0g[:], in0=r0[:], scalar=st0[:, 0:1], in1=ga_rep[:],
                                           op0=ALU.subtract, op1=ALU.mult).then_inc(centred_ready, 1)
                if a is not None:
                    normalised(0)
                if c is not None:
                    wait(dve, (ykeep_ready, c))
                    dve.wait_ge(centred_ready, c + 1)
                    dve.wait_ge(rstd0_ready, c + 1)
                    then(V.scalar_tensor_tensor(out=y[:], in0=t0g[:], scalar=st0[:, 3:4], in1=be_rep[:],
                                                op0=ALU.mult, op1=ALU.add), cross_steps, "y", c)
                    V.tensor_tensor_reduce(out=ysq[:], in0=y[:], in1=y[:], scale=1.0 / D, scalar=RMS_EPS, op0=ALU.mult, op1=ALU.add,
                                           accum_out=st0[:, 4:5]).then_inc(ms0_ready, 1)
                if a is not None:
                    normalised(1)
                if c is not None:
                    if not first(c):
                        wait(dve, self_filled("xnT", c - 1))
                    dve.wait_ge(rms0_ready, c + 1)
                    V.tensor_scalar(xn[:], y[:], st0[:, 6:7], None, ALU.mult).then_inc(xn_ready, 1)
                if a is not None:
                    normalised(2)
                    normalised(3)
                    wait(dve, self_filled("out", a))
                    dve.wait_ge(ykeep_ready, a + 1)
                    wait(dve, (x1b_ready, a))
                    V.tensor_tensor(x1[:], self_at("out")[:, 0:D], y_keep[:], ALU.add).then_inc(x1_ready, 1)
                    dve.wait_ge(x1_ready, a + 1)
                    V.tensor_tensor_reduce(out=x1sq[:], in0=x1[:], in1=x1[:], scale=1.0 / D, scalar=RMS_EPS, op0=ALU.mult, op1=ALU.add,
                                           accum_out=st1[:, 0:1]).then_inc(ms1_ready, 1)
                    if not first(a):
                        wait(dve, ff_filled("hnT", a - 1))
                    dve.wait_ge(rms1_ready, a + 1)
                    V.tensor_scalar(hn[:], x1[:], st1[:, 2:3], None, ALU.mult).then_inc(hn_ready, 1)

            pipeline(dve, body)

        @block.tensor
        def _(pe):
            mm = partial(nc.tensor.matmul, start=True, stop=True, skip_group_check=True)

            bank = lambda n: psum[:, n, :]
            pe.wait_ge(ctx_all_in, 16)
            pe.wait_ge(zeros_set, 2)
            for b in range(B):
                last = mm(bank(0)[:, b:b + 1], ctx_all[:, b, :], ones[:])
            last.then_inc(setup_pe, 1)
            pe.wait_ge(w_in, WEIGHTS_IN)
            pe.wait_ge(setup_act, 1)
            nc.tensor.transpose(bank(1)[0:B, 0:D], pool_T[:], ident[:]).then_inc(setup_pe, 1)
            pe.wait_ge(setup_dve, 4)
            nc.tensor.transpose(bank(2)[:, 0:B], pool_n[:, 2, :], ident[0:B, 0:B]).then_inc(setup_pe, 1)
            pe.wait_ge(setup_act, 2)
            mm(bank(3)[:, 0:B], wmem[:], pool_nT[:]).then_inc(setup_pe, 1)
            pe.wait_ge(setup_act, 3)
            for n in range(PAIRS):
                mm(bank(4)[:, B * n:B * (n + 1)], wqkv[:, INNER + 128 * n:INNER + 128 * (n + 1)], memT[:])
            for t in range(2):
                mm(bank(5 + t)[0:B, :], memT[:], wqkv[:, 2 * INNER + BANK * t:2 * INNER + BANK * (t + 1)])
            for n in range(PAIRS):
                last = nc.tensor.transpose(bank(7)[:, NPM * n:NPM * (n + 1)], pm_sb[:, 128 * n:128 * (n + 1)], ident[0:NPM, 0:NPM])
            last.then_inc(setup_pe, 1)
            pe.wait_ge(setup_act, 7)
            pe.wait_ge(consts_cast, 1)
            pe.wait_ge(pm_v_in, 16 * NSEG)

            q_hi = qpad[:].bitcast(BF16).rearrange("p c s h (i t) -> p c s h i t", t=2)[:, :, :, :, :, 1]
            k_hi = kall[:].bitcast(BF16).rearrange("p c s (k t) -> p c s k t", t=2)[:, :, :, :, 1]
            v0_flat = v0[:].rearrange("k g r w -> k (g r w)")

            def body(c, a, f):
                def project(name):
                    lo = INNER * "qkv".index(name[0]) + BANK * int(name[1])
                    wait(pe, self_free(name, a))
                    mm(self_at(name), xnT[:], wqkv[:, lo:lo + BANK]).then_inc(self_fill(name), 1)

                def scores(t):
                    wait(pe, self_free(f"score{t}", a))
                    for n in range(4):
                        pair, s = 2 * t + n // 2, n % 2
                        mm(self_at(f"score{t}")[0:KEYS, 128 * n:128 * (n + 1)], kall[:, pair, s, :],
                           qpad[:, pair, s, :, :].rearrange("p h i -> p (h i)"), start=n == 0, stop=False)

                def less_maxima(t):
                    for n in range(4):
                        pair, s = 2 * t + n // 2, n % 2
                        p = self_at(f"score{t}")[0:KEYS, 128 * n:128 * (n + 1)]
                        for h in range(2):
                            last = mm(p[:, SEG * h:SEG * (h + 1)], select_b[:, (2 * pair + h) * NSEG + s, :], shift_b[:], start=False)
                    last.then_inc(self_fill(f"score{t}"), 1)

                def weigh(t):
                    for n in range(4):
                        pair, h = 2 * t + n // 2, n % 2
                        for s in range(NSEG):
                            w = VW * (4 * t + n)
                            last = mm(self_at(f"pv{t}")[SEG * s:SEG * (s + 1), PVN * n:PVN * (n + 1)],
                                      probs[:, pair, s, h, :], vall[s][:, w:w + PVN])
                    last.then_inc(self_fill(f"pv{t}"), 1)

                def turn_heads(t):
                    pe.wait_ge(o_ready, a * 4 + (2 * t + 2))
                    for n in range(4):
                        pair = 4 * t + n
                        last = nc.tensor.transpose(self_at(f"oT{t}")[:, 128 * n:128 * (n + 1)],
                                                   o[:, 2 * pair:2 * pair + 2, :].rearrange("n h d -> n (h d)"), ident[:])
                    last.then_inc(self_fill(f"oT{t}"), 1)

                if a is not None:
                    wait(pe, self_free("xnT", a))
                    pe.wait_ge(xn_ready, a + 1)
                    nc.tensor.transpose(self_at("xnT")[:, 0:S], xn[:], ident[:]).then_inc(self_fill("xnT"), 1)
                if c is not None:
                    wait(pe, cross_free("inT", c))
                    pe.wait_ge(x_in, (c + 1) * 16)
                    pe.wait_ge(ctx_loaded, (c + 1) * 16)
                    pe.wait_ge(mask_in, (c + 1) * 16)
                    p = cross_at("inT")
                    nc.tensor.transpose(p[:, 0:S], x_sb[:], ident[:])
                    nc.tensor.transpose(p[:, S:S + S2], ctx_sb[:], ident[0:S2, 0:S2])
                    nc.tensor.transpose(p[0:S2, 256:256 + S], mask_sb[:], ident[:]).then_inc(cross_fill("inT"), 1)
                if a is not None:
                    pe.wait_ge(xnT_ready, a + 1)
                    project("q0")
                    project("k0")
                if c is not None:
                    wait(pe, cross_free("qkv", c))
                    pe.wait_ge(inT_ready, c + 1)
                    p = cross_at("qkv")
                    mm(p[:, 0:S], wq[:], xT[:])
                    mm(p[:, S:S + S2], wk[:], ctxT[:])
                    mm(p[0:S2, 256:256 + D], ctxT[:], wv[:]).then_inc(cross_fill("qkv"), 1)
                if a is not None:
                    project("v0")
                    project("q1")
                    project("k1")
                if f is not None:
                    wait(pe, ff_free("hnT", f))
                    pe.wait_ge(hn_ready, f + 1)
                    nc.tensor.transpose(ff_at("hnT")[:, 0:S], hn[:], ident[:]).then_inc(ff_fill("hnT"), 1)
                if a is not None:
                    project("v1")
                if f is not None:
                    pe.wait_ge(hnT_ready, f + 1)
                    for name, part in (("gate", 1), ("lin", 0)):
                        wait(pe, ff_free(name, f))
                        for n in range(FCH):
                            lo = DFF * part + 128 * n
                            last = mm(ff_at(name)[0:FROWS[n], S * n:S * (n + 1)], w1[:, lo:lo + FROWS[n]], hnT[:])
                        last.then_inc(ff_fill(name), 1)
                if c is not None:
                    pe.wait_ge(qkv0_ready, c + 1)
                    for t in range(4):
                        wait(pe, cross_free(f"score{t}", c))
                        for n in range(4):
                            last = mm(cross_at(f"score{t}")[0:S2, S * n:S * (n + 1)], kpad[:, 4 * t + n, :], q0T[:])
                        last.then_inc(cross_fill(f"score{t}"), 1)
                if a is not None:
                    for t, name in enumerate(QK):
                        wait(pe, self_free(f"{name}T", a))
                        pe.wait_ge(rot_ready, a * 4 + (t + 1))
                        lo = columns(name).start
                        for n in range(4):
                            last = nc.tensor.transpose(self_at(f"{name}T")[:, 128 * n:128 * (n + 1)],
                                                       ra[:, lo + 128 * n:lo + 128 * (n + 1)], ident[:])
                        last.then_inc(self_fill(f"{name}T"), 1)
                if f is not None:
                    wait(pe, ff_free("down", f))
                    pe.wait_ge(sT_ready, f + 1)
                    for n in range(FCH):
                        m = FROWS[n]
                        last = mm(ff_at("down")[:, 0:D], sT[0:m, n, :], w2[0:m, n, :], start=n == 0, stop=n == FCH - 1)
                    last.then_inc(ff_fill("down"), 1)
                if c is not None:
                    wait(pe, cross_free("pv", c))
                    for g in (0, 2):
                        pe.wait_ge(exp0_ready, c * 4 + (g + 2))
                        for r in range(4):
                            for gg in (g, g + 1):
                                half, q = 64 * (gg % 2), slice(S * (gg // 2), S * (gg // 2 + 1))
                                last = mm(cross_at("pv")[half:half + 64, q], v0_flat[:, 4 * VB * gg + 64 * r:4 * VB * gg + 64 * r + 64],
                                          z0[:, 4 * gg + r, :], start=r == 0, stop=r == 3)
                    last.then_inc(cross_fill("pv"), 1)
                if a is not None:
                    pe.wait_ge(qk_ready, a * 4 + 4)
                    pe.wait_ge(memk_ready, a + 1)
                    for t in range(4):
                        p = self_at(f"max{t}")[:, 0:4 * KEYS].rearrange("n (h k) -> n h k", h=4)
                        mm(p[:, :, 0:SEG], ident_b[:], causal_b[:].unsqueeze(1).broadcast_to([128, 4, SEG]), stop=False)
                        for n in range(4):
                            pair, h = 2 * t + n // 2, n % 2
                            for s in range(NSEG):
                                last = mm(p[SEG * s:SEG * (s + 1), n, :], q_hi[:, pair, s, h, :], k_hi[:, pair, s, :], start=False)
                        last.then_inc(self_fill(f"max{t}"), 1)
                    for t in range(3):
                        scores(t)
                if c is not None:
                    wait(pe, cross_free("wo", c))
                    pe.wait_ge(c0T_ready, c + 1)
                    mm(cross_at("wo")[:, 0:D], c0T[:], wo[:]).then_inc(cross_fill("wo"), 1)
                if a is not None:
                    pe.wait_ge(mt_ready, a + 1)
                    mm(self_at("shift")[0:64, 0:SEG], mt[:].rearrange("n s t h -> n (s t h)"), stack_b[:]).then_inc(self_fill("shift"), 1)
                    pe.wait_ge(shift_ready, a + 1)
                    for t in range(3):
                        less_maxima(t)
                    scores(3)
                    less_maxima(3)
                    pe.wait_ge(v_ready, a * 2 + 2)
                    pe.wait_ge(memv_in, a * 32 + 32)
                    pe.wait_ge(probs_ready, a * 4 + 2)
                    weigh(0)
                    pe.wait_ge(probs_ready, a * 4 + 3)
                    weigh(1)
                    weigh(2)
                    pe.wait_ge(probs_ready, a * 4 + 4)
                    weigh(3)
                    turn_heads(0)
                    turn_heads(1)
                    for n in range(PAIRS):
                        if n % 4 == 0:
                            pe.wait_ge(oT_ready, a * 2 + (n // 4 + 1))
                        last = mm(self_at("out")[:, 0:D], oT[:, n, :], wout[:, n, :], start=n == 0, stop=n == PAIRS - 1)
                    last.then_inc(self_fill("out"), 1)

            pipeline(pe, body)
    return nc


def constants():
    f = np.float32
    inv = (f(1.0) / f(10000.0) ** (np.arange(0, DH, 2, dtype=f) / f(DH))).astype(f)
    ang = (np.arange(S, dtype=f)[:, None] * inv[None, :]).astype(f).astype(np.float64)
    cos, sin = np.cos(ang), np.sin(ang)
    rope = np.stack([np.repeat(cos, 2, 1), np.stack([-sin, sin], -1).reshape(S, DH)], 1).astype(f)
    headmask = (np.arange(D)[:, None] // HD0 == np.arange(H)[None, :]).astype(f)
    i = np.arange(SEG)
    causal = np.tile(np.where(i[None, :] > i[:, None], NEG, 0.0), (NSEG, 1)).astype(f)
    stack = np.tile(np.eye(SEG), (NSEG, 1)).astype(f)
    shift = np.concatenate([np.zeros((64, SEG)), np.where(i[:, None] > i[None, :], NEG, 0.0)]).astype(f)
    select = np.zeros((128, H, NSEG, KEYS), f)
    for s in range(NSEG):
        for part in range(2):
            for h in range(H):
                select[s * 32 + part * 16 + h, h, s, :] = 1.0
    for j in range(SEG):
        select[64 + j, :, :, j] = 1.0
    return {"c_ident": np.eye(128, dtype=f), "c_rope": rope, "c_headmask": headmask, "c_causal": causal,
            "c_shift": shift, "c_select": select.reshape(128, -1), "c_stack": stack}


INPUTS = ["x", "ctx_1024", "mask_Bx1xSxS2_fk0"] + [f"L0_xattn_{n}" for n in ("Wq", "bq", "Wk", "bk", "Wv", "bv", "Wo", "bo", "gamma", "beta")] + [
    f"L1_xattn_{n}" for n in ("attn_norm_w", "to_qkv_w", "to_out_w", "persist_mem", "mem_pool_norm_w", "to_mem_tokens_w",
                              "ff_norm_w", "ff_w1", "ff_b1", "ff_w2", "ff_b2")]


def kernel(**inputs):
    import concourse.bacc as bacc
    from concourse.bass_utils import run_bass_kernel_spmd

    nc = bacc.Bacc("TRN2", target_bir_lowering=False, num_devices=1)
    arrays, args = {}, []
    for name, value in [(n, inputs[n]) for n in INPUTS] + list(constants().items()):
        value = np.ascontiguousarray(value)
        arrays[f"in_{name}"] = value
        args.append(nc.dram_tensor(f"in_{name}", value.shape, mybir.dt.from_np(value.dtype), kind="ExternalInput").ap())
    out = nc.dram_tensor("out", (B, S, D), F32, kind="ExternalOutput").ap()
    build(nc, *args, out)
    return run_bass_kernel_spmd(nc, [arrays], core_ids=[0]).results[0]["out"]
```

```python
from contextlib import ExitStack
from functools import partial

import numpy as np

import concourse.bass as bass
from concourse import mybir

ALU = mybir.AluOpType
ACT = mybir.ActivationFunctionType
F32 = mybir.dt.float32
BF16 = mybir.dt.bfloat16
F32R = mybir.dt.float32r
AX_X = mybir.AxisListType.X

B, S, D = 64, 128, 128
S2 = 77
H = 16
HD0 = D // H
GROUP = 4
DH = 64
INNER = H * DH
PAIRS = H // 2
SEG = 64
NSEG = S // SEG
NPM, NM = 16, 16
PRE = 1 + NPM
KEYS = SEG + PRE
VW = DH + 1
DFF = 341
FCH = 3
FROWS = [128, 128, DFF - 256]
LN_EPS, RMS_EPS = 1e-5, 1.1920929e-07
CLAMP = 50.0
BANK = 512
NEG = -1e30
CHUNKS = 4
QK = ("q0", "k0", "q1", "k1")


def banks(ctx, nc, psum, stage, first_bank, n_banks, tasks, same_bank=()):
    names = [t[0] for t in tasks]
    steps_on = [n > 0 and name not in same_bank for n, name in enumerate(names)]
    place = [sum(steps_on[:n + 1]) % n_banks for n in range(len(names))]
    fills = [ctx.enter_context(nc.semaphore(f"{stage}_bank{first_bank + n}_filled")) for n in range(n_banks)]

    def in_bank_of(task):
        n = names.index(task)
        users = [m for m in range(len(names)) if place[m] == place[n]]
        return users, users.index(n)

    def at(task):
        return psum[:, first_bank + place[names.index(task)], :]

    def fill(task):
        return fills[place[names.index(task)]]

    def is_filled(task, seq):
        users, position = in_bank_of(task)
        return fill(task), seq * len(users) + (position + 1)

    def is_free(task, seq):
        users, position = in_bank_of(task)
        _, read, k, per_seq = tasks[users[position - 1]]
        if position > 0:
            return read, seq * per_seq + k
        return read, 0 if first(seq) else seq * per_seq + (k - per_seq)

    return at, fill, is_filled, is_free


def steps(semaphore, *names):
    return semaphore, lambda name, seq: seq * len(names) + (names.index(name) + 1)


def wait(eng, signal_count):
    signal, count = signal_count
    if not (isinstance(count, int) and count <= 0):
        eng.wait_ge(signal, count)


def passed(eng, signal):
    eng.sem_inc(signal, 1)


def first(seq):
    return isinstance(seq, int) and seq == 0


def build(nc, seq_pack, mask_t, ctx_in, cross_pack, cols_pack, rows_pack, to_qkv_w, to_out_w, persist_mem, to_mem_tokens_w, ff_w1, ff_w2,
          c_rope, c_tables, c_select, out):
    with ExitStack() as ctx:
        def sb(name, shape, dt=F32):
            return ctx.enter_context(nc.sbuf_tensor(name, shape, dt))

        def sem(name):
            return ctx.enter_context(nc.semaphore(name))

        psum = ctx.enter_context(nc.psum_tensor("psum", [128, 8, BANK], F32))
        memv_dram = nc.dram_tensor("memv_dram", (B, INNER), F32, kind="Internal").ap()

        cross_w = sb("cross_w", [128, 5 * D + 2 * GROUP])
        wq, wk, wv, wo, ident = (cross_w[:, D * n:D * (n + 1)] for n in range(5))
        wqkv = sb("wqkv", [D, 3 * INNER])
        wqkv_hi, wqkv_lo = (sb(n, [D, 3 * INNER], F32R) for n in ("wqkv_hi", "wqkv_lo"))
        wout = sb("wout", [128, PAIRS, D])
        wmem = sb("wmem", [D, D])
        w1 = sb("w1", [D, 2 * DFF])
        w2 = sb("w2", [128, FCH, D])
        cols = sb("cols", [128, 6 + 2 * FCH])
        BQ, BK, BV, NW, PW, FW = range(6)
        ff_bias = cols[:, 6:].rearrange("p (a c) -> p a c", a=2)
        half_bg = sb("half_bg", [128, FCH])
        rows = sb("rows", [128, 4, D])
        bo_rep, ga_rep, be_rep, b2_rep = (rows[:, n, :] for n in range(4))
        ident_b = sb("ident_b", [128, 128], BF16)
        rope = sb("rope", [128, 2, DH])
        headmask = cross_w[:, 5 * D:].rearrange("p (a b) -> p a b", a=2)
        head_bias = sb("head_bias", [128, 2, GROUP])
        causal_b = sb("causal_b", [128, SEG], BF16)
        select_b = sb("select_b", [128, H * NSEG, KEYS], BF16)
        stack_b = sb("stack_b", [128, SEG], BF16)
        shift_b = sb("shift_b", [128, SEG], BF16)

        seq_in = sb("seq_in", [128, S + S2 + D])
        xT, ctxT, x_sb = seq_in[:, 0:S], seq_in[:, S:S + S2], seq_in[:, S + S2:]
        maskT = sb("maskT", [S2, S])
        wT = sb("wT", [S2, S])
        xb = sb("xb", [S, D])
        q0T = sb("q0T", [D, S])
        k0T = sb("k0T", [D, S2])
        q0T_hi, k0T_hi = sb("q0T_hi", [D, S], F32R), sb("k0T_hi", [D, S2], F32R)
        q0T_rest, k0T_rest = sb("q0T_rest", [D, S]), sb("k0T_rest", [D, S2])
        qmask_hi, qmask_lo = (sb(n, [D, GROUP, S], F32R) for n in ("qmask_hi", "qmask_lo"))
        kmask_hi, kmask_lo = (sb(n, [D, GROUP, S2], F32R) for n in ("kmask_hi", "kmask_lo"))
        VB = 4 * HD0 + 40
        v0 = sb("v0", [S2, 4, 4, VB])
        z0 = sb("z0", [S2, H, S])
        rden0 = sb("rden0", [128, 2, S])
        c0T = sb("c0T", [D, S])
        r0 = sb("r0", [S, D])
        t0g = sb("t0g", [S, D])
        y = sb("y", [S, D])
        ysq = sb("ysq", [S, D])
        xn = sb("xn", [S, D])
        st0 = sb("st0", [S, 16])
        bn0 = sb("bn0", [S, 6])

        y_keep = sb("y_keep", [S, D])
        xnT_hi, xnT_lo = sb("xnT_hi", [D, S], F32R), sb("xnT_lo", [D, S], F32R)
        ra = sb("ra", [S, 2 * INNER])
        rb = sb("rb", [S, 2 * INNER])
        qpad = sb("qpad", [128, PAIRS, NSEG, 2, SEG])
        kall = sb("kall", [128, PAIRS, NSEG, KEYS])
        memk = sb("memk", [128, B, PAIRS])
        vall = [sb(f"vall{s}", [KEYS, H * VW]) for s in range(NSEG)]
        mx = sb("mx", [128, PAIRS * NSEG])
        mt = sb("mt", [128, 2, 2, PAIRS * NSEG], BF16)
        probs = sb("probs", [KEYS, PAIRS, NSEG, 2, SEG])
        rden1 = sb("rden1", [S, H])
        o = sb("o", [S, H, DH])
        oT = sb("oT", [128, PAIRS, S])
        x1 = sb("x1", [S, D])
        x1sq = sb("x1sq", [S, D])
        hn = sb("hn", [S, D])
        st1 = sb("st1", [S, 8])

        hnT = sb("hnT", [D, S])
        half_gate = sb("half_gate", [128, FCH, S])
        tanh_gate = sb("tanh_gate", [128, FCH, S])
        ug = sb("ug", [128, FCH, S])
        sT = sb("sT", [128, FCH, S])
        x1b = sb("x1b", [S, D])
        out_sb = sb("out_sb", [S, D])

        HALF = (S2 + 1) // 2
        ctx_all = sb("ctx_all", [2 * B, HALF, D])
        ctx_sums = sb("ctx_sums", [2 * B, CHUNKS + 1, D])
        stage = sb("stage", [128, H * NSEG * KEYS])
        stage2 = sb("stage2", [128, 3 * SEG])
        table_in = sb("table_in", [1, 1])
        nhalf = sb("nhalf", [128, 1])
        pm_sb = sb("pm_sb", [NPM, INNER])
        pool_n = sb("pool_n", [B, 3, D])
        pool_st = sb("pool_st", [B, 4])
        pool_nT = sb("pool_nT", [D, B])
        memT = sb("memT", [D, B])
        memv = sb("memv", [B, INNER])

        cross_w_in = sem("cross_w_in")
        w_in = sem("w_in")
        ctx_all_in = [sem(f"ctx_all{k}_in") for k in range(CHUNKS)]
        ctx_sums_step = sem("ctx_sums_step")
        wqkv_in = sem("wqkv_in")
        pm_v_in = sem("pm_v_in")
        nhalf_set = sem("nhalf_set")
        zeros_step = sem("zeros_step")
        zeros_set = sem("zeros_set")
        wqkv_hi_ready = sem("wqkv_hi_ready")
        wqkv_lo_ready = sem("wqkv_lo_ready")
        consts_cast = sem("consts_cast")
        setup_pe, setup_act, setup_dve, setup_pool = sem("setup_pe"), sem("setup_act"), sem("setup_dve"), sem("setup_pool")
        memv_stored = sem("memv_stored")
        dve_passed, pool_passed, sp_passed = sem("dve_passed"), sem("pool_passed"), sem("sp_passed")
        inputs_in = sem("inputs_in")
        wT_ready = sem("wT_ready")
        xb_ready = sem("xb_ready")
        qk0_ready = sem("qk0_ready")
        qkv0_ready = sem("qkv0_ready")
        rest0_step = sem("rest0_step")
        lo0_ready = sem("lo0_ready")
        z_ready = sem("z_ready")
        clip_ready = sem("clip_ready")
        exp0_ready = sem("exp0_ready")
        c0T_ready = sem("c0T_ready")
        var0_ready, rstd0_ready = sem("var0_ready"), sem("rstd0_ready")
        ms0_ready, rms0_ready = sem("ms0_ready"), sem("rms0_ready")
        ms1_ready, rms1_ready = sem("ms1_ready"), sem("rms1_ready")
        centred_ready = sem("centred_ready")
        r_ready = sem("r_ready")
        xn_ready = sem("xn_ready")
        cross_step = sem("cross_step")
        ykeep_ready = sem("ykeep_ready")
        xnT_lo_ready = sem("xnT_lo_ready")
        xnT_hi_ready = sem("xnT_hi_ready")
        rope_ready = sem("rope_ready")
        rot_ready = sem("rot_ready")
        q_ready = sem("q_ready")
        k_ready = sem("k_ready")
        memk_ready = sem("memk_ready")
        memv_in = sem("memv_in")
        v_ready = sem("v_ready")
        max_ready = sem("max_ready")
        mt_ready = sem("mt_ready")
        shift_ready = sem("shift_ready")
        probs_ready = sem("probs_ready")
        o_ready = sem("o_ready")
        oT_ready = sem("oT_ready")
        x1_ready = sem("x1_ready")
        hn_ready = sem("hn_ready")
        self_step = sem("self_step")
        hnT_ready = sem("hnT_ready")
        x1b_ready = sem("x1b_ready")
        gate_ready = sem("gate_ready")
        sT_ready = sem("sT_ready")
        tanh_step = sem("tanh_step")
        silu_ready = sem("silu_ready")
        out_ready = sem("out_ready")
        out_stored = sem("out_stored")

        cross_at, cross_fill, cross_filled, cross_free = banks(ctx, nc, psum, "cross", 0, 2, [
            ("qkv", qkv0_ready, 1, 1), *[(f"score{t}", z_ready, t + 1, 4) for t in range(4)],
            ("pv0", c0T_ready, 1, 2), ("pv1", c0T_ready, 2, 2), ("wo", r_ready, 1, 1)])
        self_at, self_fill, self_filled, self_free = banks(ctx, nc, psum, "self", 2, 4, [
            ("xnT", xnT_lo_ready, 1, 1), ("q0", rope_ready, 1, 4), ("k0", rope_ready, 2, 4), ("v0", v_ready, 1, 2),
            ("q1", rope_ready, 3, 4), ("k1", rope_ready, 4, 4),
            *[(f"{name}T", q_ready if name[0] == "q" else k_ready, int(name[1]) + 1, 2) for name in QK],
            ("v1", v_ready, 2, 2),
            *[(f"max{t}", max_ready, t + 1, 4) for t in range(4)],
            *[(f"score{t}", probs_ready, t + 1, 4) for t in range(3)],
            ("shift", shift_ready, 1, 1), ("score3", probs_ready, 4, 4),
            *[(f"pv{t}", o_ready, t + 1, 4) for t in range(4)]], same_bank=("score3",))
        ff_at, ff_fill, ff_filled, ff_free = banks(ctx, nc, psum, "ff", 6, 2, [
            *[(f"oT{t}", oT_ready, t + 1, 2) for t in range(2)], ("out", x1_ready, 1, 1), ("hnT", hnT_ready, 1, 1), ("gate", gate_ready, 1, 1), ("lin", sT_ready, 1, 1), ("down", out_ready, 1, 1)])
        cross_steps = steps(cross_step, "rden0", "rden1", "bn", "mean", "y")
        self_steps = steps(self_step, "hi", *[f"rden{t}" for t in range(4)])

        cross_loads = [(cross_w[:], cross_pack), (cols[:], cols_pack),
                       (rows[:].rearrange("p n d -> p (n d)"), rows_pack.rearrange("(a n) d -> a (n d)", a=1).broadcast_to([128, 4 * D]))]
        weight_loads = [
            (wmem[:], to_mem_tokens_w), (stage2[:], c_tables),
            (pm_sb[:].rearrange("n (h d) -> n h d", h=H), persist_mem.rearrange("h n d -> n h d")),
            (rope[:], c_rope), (stage[:], c_select), (wout[:], to_out_w.rearrange("(c p) n -> p c n", p=128)), (w1[:], ff_w1),
            (w2[:, 0:2, :], ff_w2[0:256, :].rearrange("(c p) n -> p c n", p=128)), (w2[0:FROWS[2], 2, :], ff_w2[256:DFF, :]),
        ]
        CROSS_WEIGHTS_IN, WEIGHTS_IN = 16 * len(cross_loads), 16 * len(weight_loads)
        chunk = [slice(HALF * k // CHUNKS, HALF * (k + 1) // CHUNKS) for k in range(CHUNKS)]

        def columns(name):
            lo = INNER * (name[0] == "k") + BANK * int(name[1])
            return slice(lo, lo + BANK)

        block = ctx.enter_context(nc.Block())

        def pipeline(eng, body, rest_of_setup=lambda: None):
            body(0, None, None)
            rest_of_setup()
            body(1, 0, None)
            body(2, 1, 0)
            with eng.Fori(1, B - 2) as i:
                body(i + 2, i + 1, i)
            body(None, B - 1, B - 2)
            body(None, None, B - 1)

        @block.sync
        def _(sp):
            for dst, src in cross_loads:
                sp.dma_start(dst, src).then_inc(cross_w_in, 16)

            def rest_of_setup():
                sp.dma_start(wqkv[:], to_qkv_w).then_inc(wqkv_in, 16)
                for k, tokens in enumerate(chunk):
                    for half in range(2):
                        n = min(tokens.stop, S2 - HALF * half) - tokens.start
                        lo = HALF * half + tokens.start
                        sp.dma_start(ctx_all[B * half:B * (half + 1), tokens.start:tokens.start + n, :],
                                     ctx_in[:, lo:lo + n, :]).then_inc(ctx_all_in[k], 16)
                for dst, src in weight_loads:
                    sp.dma_start(dst, src).then_inc(w_in, 16)
                sp.wait_ge(zeros_set, 3)
                for s in range(NSEG):
                    sp.dma_start(vall[s][SEG + 1:KEYS, 0:H * VW].rearrange("n (h w) -> n h w", h=H)[:, :, 0:DH],
                                 persist_mem.rearrange("h n d -> n h d")).then_inc(pm_v_in, 16)

            def store(f):
                sp.wait_ge(out_ready, f + 1)
                passed(sp, sp_passed)
                sp.dma_start(out[bass.ds(f, 1), :, :].rearrange("b s d -> (b s) d"), out_sb[:]).then_inc(out_stored, 16)

            def body(c, a, f):
                if c is not None:
                    if not first(c):
                        wait(sp, cross_filled("qkv", c - 1))
                        passed(sp, sp_passed)
                    wait(sp, (xb_ready, c))
                    passed(sp, sp_passed)
                    wait(sp, (wT_ready, c))
                    passed(sp, sp_passed)
                    sp.dma_start(seq_in[:], seq_pack[bass.ds(c, 1), :, :].rearrange("b p n -> (b p) n")).then_inc(inputs_in, 16)
                    sp.dma_start(maskT[:], mask_t[bass.ds(c, 1), :, :].rearrange("b k s -> (b k) s")).then_inc(inputs_in, 16)
                if a is not None:
                    if first(a):
                        sp.wait_ge(setup_act, 4)
                        sp.dma_start(memv_dram, memv[:]).then_inc(memv_stored, 16)
                        sp.wait_ge(memv_stored, 16)
                    else:
                        wait(sp, self_filled("pv3", a - 1))
                        passed(sp, sp_passed)
                    for s in range(NSEG):
                        sp.dma_start(vall[s][SEG:SEG + 1, 0:H * VW].rearrange("n (h w) -> n h w", h=H)[:, :, 0:DH],
                                     memv_dram[bass.ds(a, 1), :].rearrange("b (h d) -> b h d", h=H)).then_inc(memv_in, 16)
                if f is not None and not first(f):
                    store(f - 1)

            pipeline(sp, body, rest_of_setup)
            store(B - 1)
            sp.wait_ge(out_stored, 16 * B)

        @block.gpsimd
        def _(pool):
            nc.gpsimd.memset(nhalf[:], -0.5).then_inc(nhalf_set, 1)
            for t in (v0, *vall, qpad, mt, half_gate, tanh_gate):
                nc.gpsimd.memset(t[:], 0.0).then_inc(zeros_step, 1)
            pool.wait_ge(zeros_step, 7)
            nc.gpsimd.memset(v0[:, :, :, 4 * HD0:5 * HD0], 1.0).then_inc(zeros_set, 1)
            for s in range(NSEG):
                nc.gpsimd.memset(vall[s][:, 0:H * VW].rearrange("n (h w) -> n h w", h=H)[:, :, DH:VW], 1.0).then_inc(zeros_step, 1)
            pool.wait_ge(zeros_step, 9)
            for s in range(NSEG):
                mem_col = vall[s][SEG:SEG + 1, 0:H * VW].rearrange("n (h w) -> n h w", h=H)[:, :, DH:VW]
                nc.gpsimd.memset(mem_col, float(NM)).then_inc(zeros_set, 1)
            pool.wait_ge(setup_dve, 1)

            def body(c, a, f):
                def rotated(name):
                    pool.wait_ge(rope_ready, a * 4 + (QK.index(name) + 1))
                    sl = columns(name)
                    nc.gpsimd.tensor_tensor(ra[:, sl], ra[:, sl], rb[:, sl], ALU.add).then_inc(rot_ready, 1)

                def lower(which):
                    rest, lo, width = ((q0T_rest, qmask_lo, S), (k0T_rest, kmask_lo, S2))[which]
                    return nc.gpsimd.tensor_tensor(lo[:], headmask[:, which, :].unsqueeze(2).broadcast_to([D, GROUP, width]),
                                                   rest[:].unsqueeze(1).broadcast_to([D, GROUP, width]), ALU.mult)

                if c is not None:
                    pool.wait_ge(qk0_ready, c + 1)
                    nc.gpsimd.tensor_tensor(q0T_rest[:], q0T[:], q0T_hi[:].bitcast(F32), ALU.subtract)
                    nc.gpsimd.tensor_tensor(k0T_rest[:], k0T[:], k0T_hi[:].bitcast(F32), ALU.subtract).then_inc(rest0_step, 1)
                    pool.wait_ge(rest0_step, c + 1)
                    lower(1)
                if f is not None:
                    pool.wait_ge(ms1_ready, f + 1)
                    nc.gpsimd.tensor_tensor(st1[:, 2:3], st1[:, 0:1], nhalf[:], ALU.pow).then_inc(rms1_ready, 1)
                if c is not None:
                    lower(0).then_inc(lo0_ready, 1)
                if a is not None:
                    if first(a):
                        pool.wait_ge(setup_dve, 4)
                        nc.gpsimd.tensor_tensor(pool_st[:, 1:2], pool_st[:, 0:1], nhalf[0:B, :], ALU.pow).then_inc(setup_pool, 1)
                    for name in QK:
                        rotated(name)
                if a is not None:
                    if first(a):
                        pool.wait_ge(setup_act, 3)
                    else:
                        wait(pool, self_filled("score3", a - 1))
                    mk = memk[:, bass.ds(a, 1), :].rearrange("p b c -> p c b").unsqueeze(2).broadcast_to([128, PAIRS, NSEG, 1])
                    nc.gpsimd.tensor_copy(kall[:, :, :, SEG:SEG + 1], mk).then_inc(memk_ready, 1)
                if f is not None:
                    pool.wait_ge(gate_ready, f + 1)
                    wait(pool, (sT_ready, f))
                    nc.gpsimd.tensor_tensor(ug[:], tanh_gate[:], half_gate[:], ALU.mult).then_inc(tanh_step, 1)
                    pool.wait_ge(tanh_step, f + 1)
                    nc.gpsimd.tensor_tensor(ug[:], ug[:], half_gate[:], ALU.add).then_inc(silu_ready, 1)
                if c is not None:
                    pool.wait_ge(inputs_in, c * 32 + 32)
                    wait(pool, (xn_ready, c))
                    nc.gpsimd.tensor_tensor(xb[:], x_sb[:], bo_rep[:], ALU.add).then_inc(xb_ready, 1)
                    if first(c):
                        pool.wait_ge(wqkv_hi_ready, 1)
                        nc.gpsimd.tensor_tensor(wqkv_lo[:], wqkv[:], wqkv_hi[:].bitcast(F32), ALU.subtract).then_inc(wqkv_lo_ready, 1)
                if a is not None:
                    pool.wait_ge(xn_ready, a + 1)
                    wait(pool, (x1_ready, a))
                    passed(pool, pool_passed)
                    nc.gpsimd.tensor_scalar(y_keep[:], y[:], 1.0, 0.0, ALU.mult, ALU.add).then_inc(ykeep_ready, 1)
                if f is not None:
                    pool.wait_ge(x1_ready, f + 1)
                    wait(pool, (out_ready, f))
                    nc.gpsimd.tensor_tensor(x1b[:], x1[:], b2_rep[:], ALU.add).then_inc(x1b_ready, 1)
                if c is not None:
                    pool.wait_ge(var0_ready, c + 1)
                    nc.gpsimd.tensor_tensor(st0[:, 3:4], st0[:, 2:3], nhalf[:], ALU.pow).then_inc(rstd0_ready, 1)
                    pool.wait_ge(ms0_ready, c + 1)
                    nc.gpsimd.tensor_tensor(st0[:, 6:7], st0[:, 4:5], nhalf[:], ALU.pow).then_inc(rms0_ready, 1)
            pipeline(pool, body)

        @block.scalar
        def _(act):
            copy = lambda out, in_, **k: nc.scalar.activation(out, in_, ACT.Copy, **k)
            bank = lambda n: psum[:, n, :]
            act.wait_ge(nhalf_set, 1)
            nc.scalar.activation(table_in[:], nhalf[0:1, :], ACT.Exp)
            act.wait_ge(cross_w_in, CROSS_WEIGHTS_IN)
            act.wait_ge(setup_dve, 1)
            act.wait_ge(zeros_set, 3)

            def rest_of_setup():
                act.wait_ge(w_in, WEIGHTS_IN)
                for n in range(FCH):
                    nc.scalar.mul(half_bg[0:FROWS[n], n:n + 1], ff_bias[0:FROWS[n], 1, n:n + 1], 0.5)

            def memory_tokens():
                act.wait_ge(setup_pe, 3)
                copy(pool_nT[:], bank(6)[:, 0:B], scale=cols[:, PW:PW + 1]).then_inc(setup_act, 1)
                act.wait_ge(setup_pe, 4)
                copy(memT[:], bank(7)[:, 0:B]).then_inc(setup_act, 1)
                act.wait_ge(setup_pe, 5)
                copy(memk[:].rearrange("p b c -> p c b"), bank(6).rearrange("p (c b) -> p c b", c=PAIRS))
                copy(memv[:, 0:BANK], bank(7)[0:B, :], scale=float(NM)).then_inc(setup_act, 1)
                act.wait_ge(setup_pe, 6)
                copy(memv[:, BANK:2 * BANK], bank(6)[0:B, :], scale=float(NM))
                pk = bank(7)[:, 0:PAIRS * NPM].rearrange("p (c n) -> p c n", c=PAIRS)
                for s in range(NSEG):
                    last = copy(kall[:, :, s, SEG + 1:KEYS], pk)
                last.then_inc(setup_act, 1)

            def body(c, a, f):
                def values(t):
                    wait(act, self_filled(f"v{t}", a))
                    for s in range(NSEG):
                        dst = vall[s][0:SEG, VW * 8 * t:VW * 8 * (t + 1)].rearrange("n (h w) -> n h w", h=8)[:, :, 0:DH]
                        last = copy(dst, self_at(f"v{t}")[SEG * s:SEG * (s + 1), :].rearrange("n (h d) -> n h d", h=8))
                    last.then_inc(v_ready, 1)

                def turned(t):
                    wait(act, self_filled(f"q{t}T", a))
                    for h in range(2):
                        rows = slice(DH * h, DH * (h + 1))
                        last = copy(qpad[rows, 4 * t:4 * t + 4, :, h, :],
                                    self_at(f"q{t}T")[rows, :].rearrange("p (c s i) -> p c s i", c=4, s=NSEG))
                    last.then_inc(q_ready, 1)

                def heads(t):
                    wait(act, ff_filled(f"oT{t}", f))
                    copy(oT[:, 4 * t:4 * t + 4, :].rearrange("p c s -> p (c s)"), ff_at(f"oT{t}")).then_inc(oT_ready, 1)

                def exp_cross(t):
                    act.wait_ge(clip_ready, c * 4 + (t + 1))
                    zt = z0[:, 4 * t:4 * t + 4, :]
                    nc.scalar.activation(zt, zt, ACT.Exp, scale=float(HD0) ** -0.5).then_inc(exp0_ready, 1)

                if a is not None:
                    wait(act, self_filled("xnT", a))
                    copy(xnT_hi[:], self_at("xnT")[:, 0:S], scale=cols[:, NW:NW + 1]).then_inc(xnT_hi_ready, 1)
                if f is not None:
                    heads(0)
                    heads(1)
                if c is not None:
                    wait(act, cross_filled("qkv", c))
                    p = cross_at("qkv")
                    for dst in (q0T, q0T_hi):
                        nc.scalar.activation(dst[:], p[:, 0:S], ACT.Identity, bias=cols[:, BQ:BQ + 1])
                    for dst in (k0T, k0T_hi):
                        last = nc.scalar.activation(dst[:], p[:, S:S + S2], ACT.Identity, bias=cols[:, BK:BK + 1])
                    last.then_inc(qk0_ready, 1)
                    for r in range(GROUP):
                        nc.scalar.activation(qmask_hi[:, r, :], p[:, 0:S], ACT.Identity,
                                             scale=headmask[:, 0, r:r + 1], bias=head_bias[:, 0, r:r + 1])
                    for g in range(GROUP):
                        nc.scalar.activation(kmask_hi[:, g, :], p[:, S:S + S2], ACT.Identity,
                                             scale=headmask[:, 1, g:g + 1], bias=head_bias[:, 1, g:g + 1])
                    copy(v0[:, :, :, 0:HD0], p[0:S2, 256:384].rearrange("k (g r d) -> k g r d", g=4, r=4)).then_inc(qkv0_ready, 1)
                if f is not None:
                    wait(act, ff_filled("hnT", f))
                    copy(hnT[:], ff_at("hnT")[:, 0:S], scale=cols[:, FW:FW + 1]).then_inc(hnT_ready, 1)
                if c is not None:
                    act.wait_ge(inputs_in, c * 32 + 32)
                    wait(act, (z_ready, c * 4))
                    copy(wT[:], maskT[:], scale=0.5, bias=0.5).then_inc(wT_ready, 1)
                if c is not None and first(c):
                    act.wait_ge(wqkv_in, 16)
                    copy(wqkv_hi[:], wqkv[:]).then_inc(wqkv_hi_ready, 1)
                if a is not None:
                    if first(a):
                        memory_tokens()
                    values(0)
                if f is not None:
                    wait(act, ff_filled("gate", f))
                    for n in range(FCH):
                        m = FROWS[n]
                        for dst, function in ((tanh_gate, ACT.Tanh), (half_gate, ACT.Identity)):
                            last = nc.scalar.activation(dst[0:m, n, :], ff_at("gate")[0:m, S * n:S * (n + 1)], function,
                                                        scale=0.5, bias=half_bg[0:m, n:n + 1])
                    last.then_inc(gate_ready, 1)
                if a is not None:
                    turned(0)
                if c is not None:
                    exp_cross(0)
                    for t in range(1, 4):
                        exp_cross(t)
                if a is not None:
                    turned(1)
                    values(1)
                    wait(act, self_filled("shift", a))
                    copy(shift_b[0:64, :], self_at("shift")[0:64, 0:SEG]).then_inc(shift_ready, 1)
                    for t in range(4):
                        wait(act, self_filled(f"score{t}", a))
                        nc.scalar.activation(probs[:, 2 * t:2 * t + 2, :, :, :].rearrange("k c s h i -> k (c s h i)"),
                                             self_at(f"score{t}")[0:KEYS, :], ACT.Exp, scale=float(DH) ** -0.5).then_inc(probs_ready, 1)
            pipeline(act, body, rest_of_setup)

        @block.vector
        def _(dve):
            V = nc.vector

            def then(ins, steps_of, name, seq):
                semaphore, done = steps_of
                ins.then_inc(semaphore, 1)
                wait(dve, (semaphore, done(name, seq)))

            dve.wait_ge(cross_w_in, CROSS_WEIGHTS_IN)
            for which, bias in ((0, BQ), (1, BK)):
                V.tensor_scalar(head_bias[:, which, :], headmask[:, which, :], cols[:, bias:bias + 1], None, ALU.mult)
            dve.wait_ge(setup_pe, 1)
            V.tensor_tensor(bo_rep[:], psum[:, 2, 256:256 + D], bo_rep[:], ALU.add).then_inc(setup_dve, 1)
            dve.wait_ge(zeros_set, 3)
            V.memset(ctx_all[B:2 * B, S2 - HALF:HALF, :], 0.0).then_inc(ctx_sums_step, 1)
            dve.wait_ge(ctx_sums_step, 1)

            def sum_tokens(k):
                dve.wait_ge(ctx_all_in[k], 32)
                V.reduce_sum(ctx_sums[:, k, :], ctx_all[:, chunk[k], :].rearrange("p s d -> p d s"), AX_X).then_inc(ctx_sums_step, 1)

            sum_tokens(0)
            sum_tokens(1)

            def rest_of_setup():
                sum_tokens(3)
                dve.wait_ge(ctx_sums_step, CHUNKS + 1)
                V.reduce_sum(ctx_sums[:, CHUNKS, :], ctx_sums[:, 0:CHUNKS, :].rearrange("p s d -> p d s"), AX_X).then_inc(setup_dve, 1)
                dve.wait_ge(w_in, WEIGHTS_IN)

            def context_means():
                dve.wait_ge(setup_pe, 2)
                V.tensor_scalar(pool_n[:, 0, :], psum[0:B, 7, 0:D], 1.0 / S2, None, ALU.mult).then_inc(setup_dve, 1)
                dve.wait_ge(setup_dve, 3)
                V.tensor_tensor_reduce(out=pool_n[:, 1, :], in0=pool_n[:, 0, :], in1=pool_n[:, 0, :], scale=1.0 / D, scalar=RMS_EPS,
                                       op0=ALU.mult, op1=ALU.add, accum_out=pool_st[:, 0:1]).then_inc(setup_dve, 1)

            def normalised_means():
                dve.wait_ge(setup_pool, 1)
                V.tensor_scalar(pool_n[:, 2, :], pool_n[:, 0, :], pool_st[:, 1:2], None, ALU.mult).then_inc(setup_dve, 1)

            def cast_tables():
                V.tensor_copy(ident_b[:], ident[:])
                V.tensor_copy(causal_b[:], stage2[:, 0:SEG])
                V.tensor_copy(stack_b[:], stage2[:, SEG:2 * SEG])
                V.tensor_copy(shift_b[:], stage2[:, 2 * SEG:3 * SEG])
                V.tensor_copy(select_b[:].rearrange("p n k -> p (n k)"), stage[:]).then_inc(consts_cast, 1)

            def body(c, a, f):
                def rotary(name):
                    wait(dve, self_filled(name, a))
                    sl = columns(name)
                    p = self_at(name).rearrange("n (h d) -> n h d", h=8)
                    V.tensor_tensor(ra[:, sl].rearrange("n (h d) -> n h d", h=8), p,
                                    rope[:, 0, :].unsqueeze(1).broadcast_to([S, 8, DH]), ALU.mult)
                    p = self_at(name).rearrange("n (h e t) -> n h e t", h=8, t=2)[:, :, :, ::-1]
                    V.tensor_tensor(rb[:, sl].rearrange("n (h e t) -> n h e t", h=8, t=2), p,
                                    rope[:, 1, :].rearrange("n (e t) -> n e t", t=2).unsqueeze(1).broadcast_to([S, 8, DH // 2, 2]),
                                    ALU.mult).then_inc(rope_ready, 1)

                def masked(t):
                    wait(dve, cross_filled(f"score{t}", c))
                    V.tensor_tensor(z0[:, 4 * t:4 * t + 4, :], cross_at(f"score{t}")[0:S2, :].rearrange("k (h q) -> k h q", h=4),
                                    wT[:].unsqueeze(1).broadcast_to([S2, 4, S]), ALU.mult).then_inc(z_ready, 1)

                def clamped(t):
                    lim = CLAMP * float(HD0) ** 0.5
                    zt = z0[:, 4 * t:4 * t + 4, :]
                    dve.wait_ge(z_ready, c * 4 + (t + 1))
                    passed(dve, dve_passed)
                    V.tensor_scalar(zt, zt, lim, -lim, ALU.min, ALU.max).then_inc(clip_ready, 1)

                def context_sums(t):
                    wait(dve, cross_filled(f"pv{t}", c))
                    V.reciprocal(rden0[:, t, :], cross_at(f"pv{t}")[:, 0:S]).then_inc(cross_step, 1)

                def context(t):
                    wait(dve, (cross_step, cross_steps[1](f"rden{t}", c)))
                    for half in (0, 64):
                        row = 64 * t + half // 2
                        last = V.tensor_tensor(c0T[row:row + 32, :], cross_at(f"pv{t}")[half:half + 32, 0:S],
                                               rden0[half + 32:half + 64, t, :], ALU.mult)
                    last.then_inc(c0T_ready, 1)

                def normalised(t):
                    wait(dve, self_filled(f"pv{t}", a))
                    p = self_at(f"pv{t}")[:, 0:4 * VW].rearrange("n (h w) -> n h w", h=4)
                    then(V.reciprocal(rden1[:, 4 * t:4 * t + 4].unsqueeze(2), p[:, :, DH:VW]), self_steps, f"rden{t}", a)
                    V.tensor_tensor(o[:, 4 * t:4 * t + 4, :], p[:, :, 0:DH],
                                    rden1[:, 4 * t:4 * t + 4].unsqueeze(2).broadcast_to([S, 4, DH]), ALU.mult).then_inc(o_ready, 1)

                if a is not None:
                    dve.wait_ge(xnT_hi_ready, a + 1)
                    V.scalar_tensor_tensor(out=xnT_lo[:], in0=self_at("xnT")[:, 0:S], scalar=cols[:, NW:NW + 1],
                                           in1=xnT_hi[:].bitcast(F32), op0=ALU.mult, op1=ALU.subtract).then_inc(xnT_lo_ready, 1)
                    rotary("q0")
                    if first(a):
                        context_means()
                if f is not None:
                    wait(dve, ff_filled("out", f))
                    dve.wait_ge(ykeep_ready, f + 1)
                    wait(dve, (x1b_ready, f))
                    V.tensor_tensor(x1[:], ff_at("out")[:, 0:D], y_keep[:], ALU.add).then_inc(x1_ready, 1)
                    dve.wait_ge(x1_ready, f + 1)
                    V.tensor_tensor_reduce(out=x1sq[:], in0=x1[:], in1=x1[:], scale=1.0 / D, scalar=RMS_EPS, op0=ALU.mult, op1=ALU.add,
                                           accum_out=st1[:, 0:1]).then_inc(ms1_ready, 1)
                if a is not None:
                    rotary("k0")
                    if first(a):
                        normalised_means()
                if f is not None:
                    if not first(f):
                        wait(dve, ff_filled("hnT", f - 1))
                    dve.wait_ge(rms1_ready, f + 1)
                    V.tensor_scalar(hn[:], x1[:], st1[:, 2:3], None, ALU.mult).then_inc(hn_ready, 1)
                if a is not None:
                    rotary("q1")
                    rotary("k1")
                    if first(a):
                        cast_tables()
                if c is not None:
                    dve.wait_ge(wT_ready, c + 1)
                    masked(0)
                    masked(1)
                    clamped(0)
                    clamped(1)
                    masked(2)
                    masked(3)
                    clamped(2)
                    clamped(3)
                    if first(c):
                        sum_tokens(2)
                if a is not None:
                    for t in range(2):
                        wait(dve, self_filled(f"k{t}T", a))
                        V.tensor_copy(kall[:, 4 * t:4 * t + 4, :, 0:SEG],
                                      self_at(f"k{t}T").rearrange("p (c s j) -> p c s j", c=4, s=NSEG)).then_inc(k_ready, 1)
                if c is not None:
                    context_sums(0)
                if a is not None:
                    for t in range(4):
                        wait(dve, self_filled(f"max{t}", a))
                        V.reduce_max(mx[:, 4 * t:4 * t + 4], self_at(f"max{t}")[:, 0:4 * KEYS].rearrange("i (n k) -> i n k", n=4),
                                     AX_X).then_inc(max_ready, 1)
                    dve.wait_ge(max_ready, a * 4 + 4)
                    for h in range(2):
                        rows = slice(SEG * h, SEG * (h + 1))
                        last = V.tensor_scalar(mt[rows, h, 0, :], mx[rows, :], -1.0, None, ALU.mult)
                    then(last, self_steps, "hi", a)
                    for h in range(2):
                        rows = slice(SEG * h, SEG * (h + 1))
                        last = V.scalar_tensor_tensor(out=mt[rows, h, 1, :], in0=mx[rows, :], scalar=-1.0, in1=mt[rows, h, 0, :],
                                                      op0=ALU.mult, op1=ALU.subtract)
                    last.then_inc(mt_ready, 1)
                if c is not None:
                    context_sums(1)
                if c is not None:
                    context(0)
                    context(1)
                if f is not None:
                    wait(dve, ff_filled("lin", f))
                    dve.wait_ge(silu_ready, f + 1)
                    for n in range(FCH):
                        m = FROWS[n]
                        last = V.scalar_tensor_tensor(out=sT[0:m, n, :], in0=ff_at("lin")[0:m, S * n:S * (n + 1)],
                                                      scalar=ff_bias[0:m, 0, n:n + 1], in1=ug[0:m, n, :], op0=ALU.add, op1=ALU.mult)
                    last.then_inc(sT_ready, 1)
                if c is not None:
                    wait(dve, cross_filled("wo", c))
                    dve.wait_ge(xb_ready, c + 1)
                    V.tensor_tensor(r0[:], cross_at("wo")[:, 0:D], xb[:], ALU.add).then_inc(r_ready, 1)
                    dve.wait_ge(r_ready, c + 1)
                    then(V.bn_stats(bn0[:], r0[:]), cross_steps, "bn", c)
                    passed(dve, dve_passed)
                    then(V.bn_aggr(st0[:, 0:2], bn0[:]), cross_steps, "mean", c)
                    V.tensor_scalar(st0[:, 2:3], st0[:, 1:2], LN_EPS, None, ALU.add).then_inc(var0_ready, 1)
                    V.scalar_tensor_tensor(out=t0g[:], in0=r0[:], scalar=st0[:, 0:1], in1=ga_rep[:],
                                           op0=ALU.subtract, op1=ALU.mult).then_inc(centred_ready, 1)
                if c is not None:
                    wait(dve, (ykeep_ready, c))
                    dve.wait_ge(centred_ready, c + 1)
                    dve.wait_ge(rstd0_ready, c + 1)
                    then(V.scalar_tensor_tensor(out=y[:], in0=t0g[:], scalar=st0[:, 3:4], in1=be_rep[:],
                                                op0=ALU.mult, op1=ALU.add), cross_steps, "y", c)
                    V.tensor_tensor_reduce(out=ysq[:], in0=y[:], in1=y[:], scale=1.0 / D, scalar=RMS_EPS, op0=ALU.mult, op1=ALU.add,
                                           accum_out=st0[:, 4:5]).then_inc(ms0_ready, 1)
                if f is not None:
                    wait(dve, ff_filled("down", f))
                    dve.wait_ge(x1b_ready, f + 1)
                    wait(dve, (out_stored, f * 16))
                    V.tensor_tensor(out_sb[:], ff_at("down")[:, 0:D], x1b[:], ALU.add).then_inc(out_ready, 1)
                if a is not None:
                    normalised(0)
                if c is not None:
                    if not first(c):
                        wait(dve, self_filled("xnT", c - 1))
                    dve.wait_ge(rms0_ready, c + 1)
                    V.tensor_scalar(xn[:], y[:], st0[:, 6:7], None, ALU.mult).then_inc(xn_ready, 1)
                if a is not None:
                    normalised(1)
                    normalised(2)
                    normalised(3)

            pipeline(dve, body, rest_of_setup)

        @block.tensor
        def _(pe):
            mm = partial(nc.tensor.matmul, start=True, stop=True, skip_group_check=True)

            bank = lambda n: psum[:, n, :]
            pe.wait_ge(cross_w_in, CROSS_WEIGHTS_IN)
            mm(bank(2)[:, 256:256 + D], cols[:, BV:BV + 1].broadcast_to([D, S]), wo[:]).then_inc(setup_pe, 1)

            def rest_of_setup():
                pe.wait_ge(w_in, WEIGHTS_IN)
                pe.wait_ge(wqkv_lo_ready, 1)

            def context_means():
                pe.wait_ge(setup_dve, 2)
                mm(bank(7)[0:B, 0:D], stage2[:, SEG:2 * SEG], ctx_sums[:, CHUNKS, :]).then_inc(setup_pe, 1)

            def memory_tokens():
                pe.wait_ge(setup_dve, 5)
                nc.tensor.transpose(bank(6)[:, 0:B], pool_n[:, 2, :], ident[0:B, 0:B]).then_inc(setup_pe, 1)
                pe.wait_ge(setup_act, 1)
                mm(bank(7)[:, 0:B], wmem[:], pool_nT[:]).then_inc(setup_pe, 1)
                pe.wait_ge(setup_act, 2)
                for n in range(PAIRS):
                    mm(bank(6)[:, B * n:B * (n + 1)], wqkv[:, INNER + 128 * n:INNER + 128 * (n + 1)], memT[:])
                mm(bank(7)[0:B, :], memT[:], wqkv[:, 2 * INNER:2 * INNER + BANK]).then_inc(setup_pe, 1)
                pe.wait_ge(setup_act, 3)
                mm(bank(6)[0:B, :], memT[:], wqkv[:, 2 * INNER + BANK:3 * INNER])
                for n in range(PAIRS):
                    last = nc.tensor.transpose(bank(7)[:, NPM * n:NPM * (n + 1)], pm_sb[:, 128 * n:128 * (n + 1)], ident[0:NPM, 0:NPM])
                last.then_inc(setup_pe, 1)

            q_upper = qpad[:].bitcast(BF16).rearrange("p c s h (i t) -> p c s h i t", t=2)[:, :, :, :, :, 1]
            k_upper = kall[:].bitcast(BF16).rearrange("p c s (k t) -> p c s k t", t=2)[:, :, :, :, 1]
            v0_flat = v0[:].rearrange("k g r w -> k (g r w)")

            def body(c, a, f):
                def project(name):
                    lo = INNER * "qkv".index(name[0]) + BANK * int(name[1])
                    wait(pe, self_free(name, a))
                    w = slice(lo, lo + BANK)
                    mm(self_at(name), xnT_hi[:], wqkv_hi[:, w], stop=False)
                    mm(self_at(name), xnT_hi[:], wqkv_lo[:, w], start=False, stop=False)
                    mm(self_at(name), xnT_lo[:], wqkv_hi[:, w], start=False).then_inc(self_fill(name), 1)

                def cross_scores(t):
                    wait(pe, cross_free(f"score{t}", c))
                    out = cross_at(f"score{t}")[0:S2, :]
                    q_hi, q_lo = (m[:].rearrange("p r i -> p (r i)") for m in (qmask_hi, qmask_lo))
                    mm(out, kmask_hi[:, t, :], q_hi, stop=False)
                    mm(out, kmask_hi[:, t, :], q_lo, start=False, stop=False)
                    mm(out, kmask_lo[:, t, :], q_hi, start=False).then_inc(cross_fill(f"score{t}"), 1)

                def weigh_cross(t):
                    wait(pe, cross_free(f"pv{t}", c))
                    pe.wait_ge(exp0_ready, c * 4 + (2 * t + 2))
                    for r in range(4):
                        for g in (2 * t, 2 * t + 1):
                            half, lo = 64 * (g % 2), 4 * VB * g + 64 * r
                            last = mm(cross_at(f"pv{t}")[half:half + 64, 0:S], v0_flat[:, lo:lo + 64],
                                      z0[:, 4 * g + r, :], start=r == 0, stop=r == 3)
                    last.then_inc(cross_fill(f"pv{t}"), 1)

                def turn(name):
                    wait(pe, self_free(f"{name}T", a))
                    pe.wait_ge(rot_ready, a * 4 + (QK.index(name) + 1))
                    lo = columns(name).start
                    for n in range(4):
                        last = nc.tensor.transpose(self_at(f"{name}T")[:, 128 * n:128 * (n + 1)],
                                                   ra[:, lo + 128 * n:lo + 128 * (n + 1)], ident[:])
                    last.then_inc(self_fill(f"{name}T"), 1)

                def scores(t):
                    wait(pe, self_free(f"score{t}", a))
                    for n in range(4):
                        pair, s = 2 * t + n // 2, n % 2
                        mm(self_at(f"score{t}")[0:KEYS, 128 * n:128 * (n + 1)], kall[:, pair, s, :],
                           qpad[:, pair, s, :, :].rearrange("p h i -> p (h i)"), start=n == 0, stop=False)

                def less_maxima(t):
                    for n in range(4):
                        pair, s = 2 * t + n // 2, n % 2
                        p = self_at(f"score{t}")[0:KEYS, 128 * n:128 * (n + 1)]
                        for h in range(2):
                            last = mm(p[:, SEG * h:SEG * (h + 1)], select_b[:, (2 * pair + h) * NSEG + s, :], shift_b[:], start=False)
                    last.then_inc(self_fill(f"score{t}"), 1)

                def weigh(t):
                    for n in range(4):
                        pair, h = 2 * t + n // 2, n % 2
                        for s in range(NSEG):
                            w = VW * (4 * t + n)
                            last = mm(self_at(f"pv{t}")[SEG * s:SEG * (s + 1), VW * n:VW * (n + 1)],
                                      probs[:, pair, s, h, :], vall[s][:, w:w + VW])
                    last.then_inc(self_fill(f"pv{t}"), 1)

                def turn_heads(t):
                    wait(pe, ff_free(f"oT{t}", f))
                    for n in range(4):
                        pair = 4 * t + n
                        if n % 2 == 0:
                            pe.wait_ge(o_ready, f * 4 + (pair // 2 + 1))
                        last = nc.tensor.transpose(ff_at(f"oT{t}")[:, 128 * n:128 * (n + 1)],
                                                   o[:, 2 * pair:2 * pair + 2, :].rearrange("n h d -> n (h d)"), ident[:])
                    last.then_inc(ff_fill(f"oT{t}"), 1)

                if a is not None:
                    wait(pe, self_free("xnT", a))
                    pe.wait_ge(xn_ready, a + 1)
                    nc.tensor.transpose(self_at("xnT")[:, 0:S], xn[:], ident[:]).then_inc(self_fill("xnT"), 1)
                if f is not None:
                    turn_heads(0)
                if c is not None:
                    wait(pe, cross_free("qkv", c))
                    pe.wait_ge(inputs_in, c * 32 + 32)
                    p = cross_at("qkv")
                    mm(p[:, 0:S], wq[:], xT[:])
                    mm(p[:, S:S + S2], wk[:], ctxT[:])
                    mm(p[0:S2, 256:256 + D], ctxT[:], wv[:]).then_inc(cross_fill("qkv"), 1)
                if f is not None:
                    turn_heads(1)
                if a is not None:
                    pe.wait_ge(xnT_lo_ready, a + 1)
                    project("q0")
                    if first(a):
                        context_means()
                if f is not None:
                    wait(pe, ff_free("out", f))
                    for n in range(PAIRS):
                        if n % 4 == 0:
                            pe.wait_ge(oT_ready, f * 2 + (n // 4 + 1))
                        last = mm(ff_at("out")[:, 0:D], oT[:, n, :], wout[:, n, :], start=n == 0, stop=n == PAIRS - 1)
                    last.then_inc(ff_fill("out"), 1)
                if a is not None:
                    project("k0")
                    project("q1")
                    project("k1")
                    project("v0")
                    if first(a):
                        memory_tokens()
                if f is not None:
                    wait(pe, ff_free("hnT", f))
                    pe.wait_ge(hn_ready, f + 1)
                    nc.tensor.transpose(ff_at("hnT")[:, 0:S], hn[:], ident[:]).then_inc(ff_fill("hnT"), 1)
                if c is not None:
                    pe.wait_ge(qkv0_ready, c + 1)
                    pe.wait_ge(lo0_ready, c + 1)
                    cross_scores(0)
                    cross_scores(1)
                if f is not None:
                    pe.wait_ge(hnT_ready, f + 1)
                    for name, part in (("gate", 1), ("lin", 0)):
                        wait(pe, ff_free(name, f))
                        for n in range(FCH):
                            lo = DFF * part + 128 * n
                            last = mm(ff_at(name)[0:FROWS[n], S * n:S * (n + 1)], w1[:, lo:lo + FROWS[n]], hnT[:])
                        last.then_inc(ff_fill(name), 1)
                if a is not None:
                    turn("q0")
                    turn("k0")
                if c is not None:
                    cross_scores(2)
                    cross_scores(3)
                if a is not None:
                    turn("q1")
                    project("v1")
                    turn("k1")
                if c is not None:
                    weigh_cross(0)
                    weigh_cross(1)
                if a is not None:
                    if first(a):
                        pe.wait_ge(setup_act, 4)
                        pe.wait_ge(consts_cast, 1)
                    pe.wait_ge(q_ready, a * 2 + 2)
                    pe.wait_ge(k_ready, a * 2 + 2)
                    pe.wait_ge(memk_ready, a + 1)
                    for t in range(4):
                        if t == 3:
                            wait(pe, self_free("max3", a))
                        p = self_at(f"max{t}")[:, 0:4 * KEYS].rearrange("i (n k) -> i n k", n=4)
                        mm(p[:, :, 0:SEG], ident_b[:], causal_b[:].unsqueeze(1).broadcast_to([128, 4, SEG]), stop=False)
                        for n in range(4):
                            pair, s = 2 * t + n // 2, n % 2
                            last = mm(p[:, n, :], q_upper[:, pair, s, :, :].rearrange("p h i -> p (h i)"),
                                      k_upper[:, pair, s, :], start=False)
                        last.then_inc(self_fill(f"max{t}"), 1)
                    scores(0)
                    scores(1)
                if a is not None:
                    wait(pe, self_free("shift", a))
                    pe.wait_ge(mt_ready, a + 1)
                    mm(self_at("shift")[0:64, 0:SEG], mt[:].rearrange("i h t n -> i (h t n)"), stack_b[:]).then_inc(self_fill("shift"), 1)
                    scores(2)
                    pe.wait_ge(shift_ready, a + 1)
                    scores(3)
                if c is not None:
                    pe.wait_ge(c0T_ready, c * 2 + 2)
                    mm(cross_at("wo")[:, 0:D], c0T[:], wo[:]).then_inc(cross_fill("wo"), 1)
                if a is not None:
                    for t in range(4):
                        less_maxima(t)
                if f is not None:
                    wait(pe, ff_free("down", f))
                    pe.wait_ge(sT_ready, f + 1)
                    for n in range(FCH):
                        m = FROWS[n]
                        last = mm(ff_at("down")[:, 0:D], sT[0:m, n, :], w2[0:m, n, :], start=n == 0, stop=n == FCH - 1)
                    last.then_inc(ff_fill("down"), 1)
                if a is not None:
                    if first(a):
                        pe.wait_ge(pm_v_in, 16 * NSEG)
                    pe.wait_ge(v_ready, a * 2 + 2)
                    pe.wait_ge(memv_in, a * 32 + 32)
                    pe.wait_ge(probs_ready, a * 4 + 2)
                    weigh(0)
                    weigh(1)
                    pe.wait_ge(probs_ready, a * 4 + 3)
                    weigh(2)
                    pe.wait_ge(probs_ready, a * 4 + 4)
                    weigh(3)
            pipeline(pe, body, rest_of_setup)
    return nc


def constants():
    f = np.float32
    inv = (f(1.0) / f(10000.0) ** (np.arange(0, DH, 2, dtype=f) / f(DH))).astype(f)
    ang = (np.arange(S, dtype=f)[:, None] * inv[None, :]).astype(f).astype(np.float64)
    cos, sin = np.cos(ang), np.sin(ang)
    rope = np.stack([np.repeat(cos, 2, 1), np.stack([-sin, sin], -1).reshape(S, DH)], 1).astype(f)
    head = np.arange(D)[:, None] // HD0
    headmask = np.concatenate([head % GROUP == np.arange(GROUP), head // GROUP == np.arange(GROUP)], 1).astype(f)
    i = np.arange(SEG)
    causal = np.tile(np.where(i[None, :] > i[:, None], NEG, 0.0), (2, 1)).astype(f)
    stack = np.tile(np.eye(SEG), (2, 1)).astype(f)
    shift = np.concatenate([np.zeros((64, SEG)), np.where(i[:, None] > i[None, :], NEG, 0.0)]).astype(f)
    select = np.zeros((128, H, NSEG, KEYS), f)
    for s in range(NSEG):
        for part in range(2):
            for h in range(H):
                select[h % 2 * 32 + part * 16 + h // 2 * NSEG + s, h, s, :] = 1.0
    for j in range(SEG):
        select[64 + j, :, :, j] = 1.0
    return {"ident": np.eye(128, dtype=f), "headmask": headmask, "rope": rope,
            "tables": np.concatenate([causal, stack, shift], 1), "select": select.reshape(128, -1)}


def layout(inputs):
    f = np.float32
    l0 = lambda *names: [inputs[f"L0_xattn_{n}"] for n in names]
    l1 = lambda *names: [inputs[f"L1_xattn_{n}"] for n in names]
    table = constants()
    ff_b1 = np.zeros((128, 2, FCH), f)
    for part, half in enumerate(np.split(l1("ff_b1")[0], 2)):
        for c in range(FCH):
            ff_b1[0:FROWS[c], part, c] = half[128 * c:128 * c + FROWS[c]]
    columns = l0("bq", "bk", "bv") + l1("attn_norm_w", "mem_pool_norm_w", "ff_norm_w")
    x, ctx_in = inputs["x"], inputs["ctx_1024"]
    seq_pack = np.concatenate([x.transpose(0, 2, 1), ctx_in.transpose(0, 2, 1), x], 2)
    return [seq_pack, inputs["mask_Bx1xSxS2_fk0"][:, 0].transpose(0, 2, 1), ctx_in,
            np.concatenate(l0("Wq", "Wk", "Wv", "Wo") + [table["ident"], table["headmask"]], 1),
            np.concatenate([np.stack(columns, 1), ff_b1.reshape(128, -1)], 1),
            np.stack(l0("bo", "gamma", "beta") + l1("ff_b2")),
            *l1("to_qkv_w", "to_out_w", "persist_mem", "to_mem_tokens_w", "ff_w1", "ff_w2"),
            table["rope"], table["tables"], table["select"]]


def kernel(**inputs):
    import concourse.bacc as bacc
    from concourse.bass_utils import run_bass_kernel_spmd

    nc = bacc.Bacc("TRN2", target_bir_lowering=False, num_devices=1)
    arrays, args = {}, []
    for n, value in enumerate(layout(inputs)):
        value = np.ascontiguousarray(value)
        arrays[f"in_{n}"] = value
        args.append(nc.dram_tensor(f"in_{n}", value.shape, mybir.dt.from_np(value.dtype), kind="ExternalInput").ap())
    out = nc.dram_tensor("out", (B, S, D), F32, kind="ExternalOutput").ap()
    build(nc, *args, out)
    return run_bass_kernel_spmd(nc, [arrays], core_ids=[0]).results[0]["out"]
```
